# Optimizing a Trainium2 kernel written in Bass

```python
import numpy as np
import jax
import jax.numpy as jnp

def _softmax(x, axis=-1):
    return jax.nn.softmax(x, axis=axis)

def _gelu(x):
    return jax.nn.gelu(x, approximate=True)

def _silu(x):
    return jax.nn.silu(x)

def _sigmoid(x):
    return jax.nn.sigmoid(x)

def _layernorm(x, axis=-1, eps=1e-05):
    m = jnp.mean(x, axis=axis, keepdims=True)
    v = jnp.var(x, axis=axis, keepdims=True)
    return (x - m) / jnp.sqrt(v + eps)

def _scatter_add(tgt, idx, src, axis=0):
    return tgt.at[idx].add(src)

def _segment_sum(src, seg, n):
    return jax.ops.segment_sum(src, seg, n)
kernel_name = 'mk_seq_preln_d1_jaxref_r8_723809'

def setup_inputs(seed: int=0):
    np.random.seed(seed)
    _w = jnp.asarray

    def _L0_attn_setup():
        import jax, jax.numpy as jnp
        import numpy as np
        DIM = 128
        B, T = (4, 512)
        CAP = 10.0
        EPS_N = 1e-06
        EPS_RMS = 1e-08

        def softcap(x, a=CAP):
            return a * jnp.tanh(x / a)
        key = jax.random.key(seed)
        k1, k2 = jax.random.split(key)
        x = jax.random.normal(k1, (B, T, DIM), dtype=jnp.float32)
        W = jax.random.normal(k2, (DIM, 4 * DIM), dtype=jnp.float32) / np.sqrt(DIM)
        b = jnp.zeros((4 * DIM,), dtype=jnp.float32)
        input_bias = -jnp.ones((DIM,), dtype=jnp.float32)
        scale = jnp.ones((DIM,), dtype=jnp.float32)
        return {'x': x, 'W': W, 'b': b, 'input_bias': input_bias, 'scale': scale}
    _L0_attn_in = _L0_attn_setup()

    def _L0_ffn_setup():
        import jax, jax.numpy as jnp
        import numpy as np
        H = 16
        TOP_K = 2
        LN_EPS = 1e-05
        key = jax.random.key(seed)
        ks = jax.random.split(key, 8)
        B, S, E, NE = (2, 128, 128, 8)
        w = lambda k, shp: jax.random.normal(k, shp, dtype=jnp.float32) * 0.02
        return {'x': jax.random.normal(ks[0], (B, S, E), dtype=jnp.float32), 'rW1': w(ks[1], (E // 2, E)), 'rb1': jnp.zeros((E // 2,), jnp.float32), 'ln_g': jnp.ones((E // 2,), jnp.float32), 'ln_b': jnp.zeros((E // 2,), jnp.float32), 'rW2': w(ks[2], (NE, E // 2)), 'rb2': jnp.zeros((NE,), jnp.float32), 'qW': w(ks[3], (NE, E, E)), 'qb': jnp.zeros((NE, E), jnp.float32), 'kW': w(ks[4], (NE, E, E)), 'kb': jnp.zeros((NE, E), jnp.float32), 'vW': w(ks[5], (NE, E, E)), 'vb': jnp.zeros((NE, E), jnp.float32), 'oW': w(ks[6], (NE, E, E)), 'ob': jnp.zeros((NE, E), jnp.float32)}
    _L0_ffn_in = _L0_ffn_setup()
    _d = {'L0_attn_x': _L0_attn_in['x'], 'L0_attn_W': _L0_attn_in['W'], 'L0_attn_b': _L0_attn_in['b'], 'L0_attn_input_bias': _L0_attn_in['input_bias'], 'L0_attn_scale': _L0_attn_in['scale'], 'L0_ffn_rW1': _L0_ffn_in['rW1'], 'L0_ffn_rb1': _L0_ffn_in['rb1'], 'L0_ffn_ln_g': _L0_ffn_in['ln_g'], 'L0_ffn_ln_b': _L0_ffn_in['ln_b'], 'L0_ffn_rW2': _L0_ffn_in['rW2'], 'L0_ffn_rb2': _L0_ffn_in['rb2'], 'L0_ffn_qW': _L0_ffn_in['qW'], 'L0_ffn_qb': _L0_ffn_in['qb'], 'L0_ffn_kW': _L0_ffn_in['kW'], 'L0_ffn_kb': _L0_ffn_in['kb'], 'L0_ffn_vW': _L0_ffn_in['vW'], 'L0_ffn_vb': _L0_ffn_in['vb'], 'L0_ffn_oW': _L0_ffn_in['oW'], 'L0_ffn_ob': _L0_ffn_in['ob']}
    _x0 = _d['L0_attn_x']
    _d['L0_attn_x'] = jax.random.normal(jax.random.fold_in(jax.random.key(seed), 1), (16, 256, 128), dtype=_x0.dtype)
    del _x0
    return _d

def reference(L0_attn_x, L0_attn_W, L0_attn_b, L0_attn_input_bias, L0_attn_scale, L0_ffn_rW1, L0_ffn_rb1, L0_ffn_ln_g, L0_ffn_ln_b, L0_ffn_rW2, L0_ffn_rb2, L0_ffn_qW, L0_ffn_qb, L0_ffn_kW, L0_ffn_kb, L0_ffn_vW, L0_ffn_vb, L0_ffn_oW, L0_ffn_ob):

    def _L0_attn_ref(x, W, b, input_bias, scale):
        import jax, jax.numpy as jnp
        import numpy as np
        DIM = 128
        B, T = (4, 512)
        CAP = 10.0
        EPS_N = 1e-06
        EPS_RMS = 1e-08

        def softcap(x, a=CAP):
            return a * jnp.tanh(x / a)
        pre = jnp.einsum('btd,df->btf', x, W) + b
        i_pre, f_pre, o_pre, z = jnp.split(pre, 4, axis=-1)
        i_gate = softcap(i_pre + input_bias)
        f_gate = -jax.nn.softplus(f_pre)
        o_sig = jax.nn.sigmoid(o_pre)
        tz = jnp.tanh(z)
        seq = (jnp.swapaxes(i_gate, 0, 1), jnp.swapaxes(f_gate, 0, 1), jnp.swapaxes(o_sig, 0, 1), jnp.swapaxes(tz, 0, 1))
        c0 = jnp.zeros((x.shape[0], DIM), dtype=x.dtype)
        n0 = jnp.zeros_like(c0)
        m0 = jnp.zeros_like(c0)

        def step(carry, inp):
            c, n, m = carry
            i_t, f_t, o_t, tz_t = inp
            m_next = jnp.maximum(f_t + m, i_t)
            i_s = jnp.exp(i_t - m_next)
            f_s = jnp.exp(f_t + m - m_next)
            c = f_s * c + i_s * tz_t
            n = f_s * n + i_s
            h = o_t * (c / (n + EPS_N))
            return ((c, n, m_next), h)
        _, hs = jax.lax.scan(step, (c0, n0, m0), seq)
        out = jnp.swapaxes(hs, 0, 1)
        rms = jnp.sqrt(jnp.mean(jnp.square(out), axis=-1, keepdims=True) + EPS_RMS)
        out = out / rms * scale
        return out

    def _L0_ffn_ref(x, rW1, rb1, ln_g, ln_b, rW2, rb2, qW, qb, kW, kb, vW, vb, oW, ob):
        import jax, jax.numpy as jnp
        import numpy as np
        H = 16
        TOP_K = 2
        LN_EPS = 1e-05
        B, S, E = x.shape
        NE = qW.shape[0]
        Dh = E // H
        scale = 1.0 / jnp.sqrt(jnp.asarray(Dh, x.dtype))
        h = x @ rW1.T + rb1
        mu = h.mean(-1, keepdims=True)
        var = ((h - mu) ** 2).mean(-1, keepdims=True)
        h = (h - mu) * jax.lax.rsqrt(var + LN_EPS) * ln_g + ln_b
        h = jax.nn.relu(h)
        logits = h @ rW2.T + rb2
        probs = jax.nn.softmax(logits, axis=-1)
        tp, ti = jax.lax.top_k(probs, TOP_K)
        tp = tp / tp.sum(-1, keepdims=True)
        expert_mask = (jax.nn.one_hot(ti, NE, dtype=probs.dtype) * tp[..., None]).sum(-2)
        gates = jnp.moveaxis(expert_mask, -1, 0)

        def expert_step(acc, params):
            qw, qb_, kw, kb_, vw, vb_, ow, ob_, g = params
            q = (x @ qw.T + qb_).reshape(B, S, H, Dh).transpose(0, 2, 1, 3)
            k = (x @ kw.T + kb_).reshape(B, S, H, Dh).transpose(0, 2, 1, 3)
            v = (x @ vw.T + vb_).reshape(B, S, H, Dh).transpose(0, 2, 1, 3)
            scores = jnp.einsum('bhqd,bhkd->bhqk', q, k) * scale
            p = jax.nn.softmax(scores, axis=-1)
            o = jnp.einsum('bhqk,bhkd->bhqd', p, v)
            o = o.transpose(0, 2, 1, 3).reshape(B, S, E) @ ow.T + ob_
            return (acc + o * g[..., None], None)
        out, _ = jax.lax.scan(expert_step, jnp.zeros_like(x), (qW, qb, kW, kb, vW, vb, oW, ob, gates))
        return out
    x = L0_attn_x
    x = x + _L0_attn_ref(_layernorm(x, axis=-1), L0_attn_W, L0_attn_b, L0_attn_input_bias, L0_attn_scale)
    x = x + _L0_ffn_ref(_layernorm(x, axis=-1), L0_ffn_rW1, L0_ffn_rb1, L0_ffn_ln_g, L0_ffn_ln_b, L0_ffn_rW2, L0_ffn_rb2, L0_ffn_qW, L0_ffn_qb, L0_ffn_kW, L0_ffn_kb, L0_ffn_vW, L0_ffn_vb, L0_ffn_oW, L0_ffn_ob)
    return x

_drawn_inputs = setup_inputs


def setup_inputs(seed=0):
    import zlib

    import numpy as np

    out = dict(_drawn_inputs(seed))
    spreads = {'L0_attn_b': (0.0, 0.1),
     'L0_attn_input_bias': (-1.0, 0.6),
     'L0_attn_scale': (1.0, 0.2),
     'L0_ffn_rb1': (0.0, 0.1),
     'L0_ffn_ln_g': (1.0, 0.6),
     'L0_ffn_ln_b': (0.0, 0.422),
     'L0_ffn_rb2': (0.0, 0.1),
     'L0_ffn_qb': (0.0, 0.8),
     'L0_ffn_kb': (0.0, 0.8),
     'L0_ffn_vb': (0.0, 0.718),
     'L0_ffn_ob': (0.0, 0.1)}
    factors = {'L0_ffn_qW': 8.0, 'L0_ffn_kW': 8.0, 'L0_ffn_vW': 8.0, 'L0_ffn_oW': 4.713}
    for name, (base, spread) in spreads.items():
        noise = np.random.default_rng([zlib.crc32(name.encode()), seed]).standard_normal(out[name].shape)
        drawn = base * np.exp(spread * noise) if base else spread * noise
        out[name] = jnp.asarray(drawn.astype(out[name].dtype))
    for name, factor in factors.items():
        out[name] = (out[name] * factor).astype(out[name].dtype)
    return out
```

```python
import concourse.bass as bass
from concourse import mybir
from contextlib import ExitStack

fp32 = mybir.dt.float32
bf16 = mybir.dt.bfloat16
ALU = mybir.AluOpType
ACT = mybir.ActivationFunctionType
AX = mybir.AxisListType

B, T, D = 16, 256, 128
TILES = B * T // 128
GROUPS = TILES // 4
GT = 4 * 128
NE, H, DH = 8, 16, 8
R = D // 2
PAIRS = H // 2
UNITS = 2 * PAIRS
CAP = 10.0
SCALE = float(DH) ** -0.5
BELOW = -3.0e38


def xlstm_moe_attention(nc, x, W, b4, ib, scale, rW1, rb1, ln_g, ln_b, rW2, rb2,
                        qW, qb, kW, kb, vW, vb, oW, ob, out):
    ctx = ExitStack()
    with ctx:
        def sb(name, shape, dt=fp32):
            return ctx.enter_context(nc.sbuf_tensor(name, shape, dt))

        def ps(name, shape):
            return ctx.enter_context(nc.psum_tensor(name, shape, fp32))

        def sem(name):
            return ctx.enter_context(nc.semaphore(name))

        w_gates = sb("w_gates", [128, 4 * D])
        b_gates = sb("b_gates", [128, 4])
        b_in = sb("b_in", [128, 1])
        b_ti = sb("b_ti", [128, 1])
        b_no = sb("b_no", [128, 1])
        scale_bc = sb("scale_bc", [128, D])
        rw1 = sb("rw1", [128, R])
        rw2 = sb("rw2", [2 * R, NE])
        rb1_bc = sb("rb1_bc", [128, R])
        lng_bc = sb("lng_bc", [128, R])
        lnb_bc = sb("lnb_bc", [128, R])
        rb2_bc = sb("rb2_bc", [128, NE])
        q_w = sb("q_w", [128, H * NE * DH])
        k_w = sb("k_w", [128, H * NE * DH])
        v_w = sb("v_w", [128, H * NE * DH])
        o_w = sb("o_w", [128, PAIRS * D])
        q_b = sb("q_b", [128, PAIRS])
        k_b = sb("k_b", [128, PAIRS])
        v_b = sb("v_b", [128, H * NE * DH])
        ob_w = sb("ob_w", [2 * 32, D])
        ident = sb("ident", [128, 128])
        eps5 = sb("eps5", [128, 1])
        eps8 = sb("eps8", [128, 1])
        rev = sb("rev", [128, NE])
        cap = sb("cap", [128, 1])

        xs = sb("xs", [128, TILES * D])
        t_i = sb("t_i", [128, B * T])
        t_z = sb("t_z", [128, B * T])
        t_o = sb("t_o", [128, B * T])
        t_f = sb("t_f", [128, B * T])
        t_a = sb("t_a", [128, B * T])
        t_m = sb("t_m", [128, B * (T + 1)])
        stats = sb("stats", [128, TILES * 6])
        mean = sb("mean", [128, TILES])[:, :]
        var = sb("var", [128, TILES])[:, :]
        rstd = sb("rstd", [128, TILES])
        spread = sb("spread", [128, TILES])[:, :]
        ssq = sb("ssq", [128, TILES])
        hr = sb("hr", [128, TILES * R])
        lg = sb("lg", [128, TILES * NE])
        gate = sb("gate", [128, 2 * TILES])
        oh = sb("oh", [128, 2 * TILES * NE])
        g8 = sb("g8", [128, TILES * 32])
        mask = sb("mask", [128, B * 512], bf16)
        st_a = [sb(f"st_a{q}", [128, GT]) for q in range(2)]
        st_b = [sb(f"st_b{q}", [128, GT]) for q in range(2)]
        sm64 = [sb(f"sm64{q}", [64, 128])[:, :] for q in range(2)]
        g_st = [sb(f"g_st{q}", [128, 64])[:, :] for q in range(2)]
        x_cur = sb("x_cur", [128, T])
        q_m = [sb(f"q_m{i}", [128, 2 * T]) for i in range(2)]
        k_m = [sb(f"k_m{i}", [128, T]) for i in range(2)]
        v_m = [sb(f"v_m{i}", [128, 2 * 128]) for i in range(4)]
        prob = [t_z[:, i * 1024:(i + 1) * 1024] for i in range(4)]
        probT = [t_o[:, i * 1024:(i + 1) * 1024] for i in range(2)]
        negmax = sb("negmax", [128, 4 * 4])
        den = sb("den", [128, 4 * 4])
        fac = sb("fac", [128, 4 * 4])
        o_m = t_o[:, 2048:2048 + 512]
        o_sum = t_f[:, 0:PAIRS * T]

        PS = [ps(f"ps{i}", [128, 512]) for i in range(4)]
        ps_s = [ps(f"ps_s{i}", [128, 1024]) for i in range(2)]

        names = """w_in w_small zero ident_ready consts x_in1 x_in2 x_in3 x_in0
        a_stats moment_step a_ln a_rstd a_xn a_tp a_xt a_gates_ps a_gates_act a_gates_dve
        b_exp b_ln b_f b_i b_m b_t b_d2 b_d1 b_fs b_is b_u b_n b_c b_ne b_d b_r b_h b_tp b_h2 b_sq
        c_ln c_rs c_h3 c_x1 c_stats c_ln2 c_rstd
        d_xn d_tp d_xt d_xt2 d_hr_ps d_hr
        e_stats e_ln e_rstd e_n e_g e_b
        f_st f_tp f_hT f_lg_ps f_lg
        t_step t_e t_ex g_st g_tp g_mask g_gT g_ob_ps g_x1
        xcur_ready qk_ps q_ready k_ready v_ps v_ready scores_ready negmax_ready probs_ready rden_ready fac_ready
        scaled_ready pT_ps pTa_ready pTb_ready pv_ps om_ready osum_ready out_ps y_ready y_out""".split()
        s = {n: sem(n) for n in names}
        block = ctx.enter_context(nc.Block())

        def v3(ap, a):
            return ap.rearrange("p (a b) -> p a b", a=a)

        def seq(tab, g, per):
            return tab[:, bass.ds(g * per, per)]

        def bc(ap, n):
            return ap.rearrange("p (a o) -> p a o", o=1).to_broadcast([ap.shape[0], ap.shape[1], n])

        @block.sync
        def _(sp):
            xv = x.rearrange("b (h p) d -> p (b h) d", p=128)
            for c in range(4):
                sp.dma_start(v3(xs[:, c * 1024:(c + 1) * 1024], 8), xv[:, c * 8:(c + 1) * 8, :]).then_inc(s[f"x_in{c}"], 16)
            sp.dma_start(q_w[:, :], qW).then_inc(s["w_in"], 16)
            sp.dma_start(k_w[:, :], kW).then_inc(s["w_in"], 16)
            sp.dma_start(v_w[:, :], vW).then_inc(s["w_in"], 16)
            sp.dma_start(o_w[:, :], oW).then_inc(s["w_in"], 16)
            sp.dma_start(v_b[:, :], vb.to_broadcast([128, H * NE * DH])).then_inc(s["w_in"], 16)
            yv = out.rearrange("b (h p) d -> p (b h) d", p=128)
            with sp.Fori(0, B) as b:
                sp.wait_ge(s["y_ready"], b + 1 + 1)
                sp.dma_start(yv[:, bass.ds(2 * b, 2), :], v3(seq(xs, b, 2 * D), 2)).then_inc(s["y_out"], 16)
            sp.wait_ge(s["y_out"], 16 * B)

        @block.gpsimd
        def _(pool):
            pool.sem_inc(s["d_xt2"], 1)
            pool.sem_inc(s["osum_ready"], 1)
            pool.memset(ident[:, :], 0.0).then_inc(s["zero"], 1)
            pool.wait_ge(s["zero"], 1)
            pool.affine_select(out=ident[:, :], in_=ident[:, :], compare_op=ALU.not_equal, fill=1.0, base=0,
                               pattern=[[-1, 128]], channel_multiplier=1).then_inc(s["ident_ready"], 1)
            pool.memset(eps5[:, :], 1e-5).then_inc(s["consts"], 1)
            pool.memset(eps8[:, :], 1e-8).then_inc(s["consts"], 1)
            pool.memset(cap[:, :], CAP).then_inc(s["consts"], 1)
            for e in range(NE):
                pool.memset(rev[:, e:e + 1], float(NE - e)).then_inc(s["consts"], 1)
            pool.memset(v3(t_m[:, :], B)[:, :, 0:1], 0.0).then_inc(s["consts"], 1)
            pool.memset(g8[:, :], 0.0).then_inc(s["consts"], 1)

            pool.wait_ge(s["consts"], 13)
            with pool.Fori(0, GROUPS) as g:
                pool.wait_ge(s["a_gates_ps"], 4 * GROUPS)
                pool.wait_ge(s["a_gates_act"], GROUPS + 1)
                i_g = seq(t_i, g, GT)
                pool.tensor_tensor(i_g, i_g, cap[:, :].to_broadcast([128, GT]), ALU.mult).then_inc(s["b_i"], 1)
                m = t_m[:, bass.ds(g * 2 * (T + 1), 2 * (T + 1))].rearrange("p (b t) -> p b t", b=2)
                f_g = v3(seq(t_f, g, GT), 2)
                count = pool.snap(2 * g + 2)
                pool.wait_ge(s["ident_ready"], 1)
                pool.wait_ge(s["b_m"], count)
                pool.tensor_tensor(f_g, f_g, m[:, :, 0:T], ALU.add).then_inc(s["b_t"], 1)
                count = pool.snap(g + 1)
                pool.wait_ge(s["ident_ready"], 1)
                pool.wait_ge(s["b_t"], count)
                pool.tensor_tensor(f_g, f_g, m[:, :, 1:T + 1], ALU.subtract).then_inc(s["b_d2"], 1)
                pool.tensor_tensor(v3(i_g, 2), v3(i_g, 2), m[:, :, 1:T + 1], ALU.subtract).then_inc(s["b_d1"], 1)
                count = pool.snap(g + 1)
                pool.wait_ge(s["ident_ready"], 1)
                pool.wait_ge(s["b_is"], count)
                z_g = seq(t_z, g, GT)
                pool.tensor_tensor(z_g, z_g, i_g, ALU.mult).then_inc(s["b_u"], 1)

            with pool.Fori(0, GROUPS // 2) as i:
                for q in range(2):
                    g = 2 * i + q
                    count = pool.snap(g + 1)
                    pool.wait_ge(s["ident_ready"], 1)
                    pool.wait_ge(s["d_xt"], count)
                    pool.tensor_copy(seq(t_i, g, GT), st_b[q][:, :]).then_inc(s["d_xt2"], 1)

            with pool.Fori(0, GROUPS) as g:
                count = pool.snap(4 * g + 4)
                pool.wait_ge(s["ident_ready"], 1)
                pool.wait_ge(s["e_n"], count)
                h_g = v3(seq(hr, g, 4 * R), 4)
                pool.tensor_tensor(h_g, h_g, lng_bc[:, :].rearrange("p (o r) -> p o r", o=1).to_broadcast([128, 4, R]),
                                   ALU.mult).then_inc(s["e_g"], 1)
            with pool.Fori(0, GROUPS) as g:
                pool.wait_ge(s["e_g"], GROUPS)
                h_g = v3(seq(hr, g, 4 * R), 4)
                pool.tensor_tensor(h_g, h_g, lnb_bc[:, :].rearrange("p (o r) -> p o r", o=1).to_broadcast([128, 4, R]),
                                   ALU.add).then_inc(s["e_b"], 1)

            pool.wait_ge(s["d_xt2"], GROUPS + 1)
            pool.tensor_copy(x_cur[:, :], t_i[:, 0:T]).then_inc(s["xcur_ready"], 1)

            def scaled(b, u):
                n = UNITS * b + u
                pool.wait_ge(s["fac_ready"], n + 1)
                for h in range(2):
                    p = v3(prob[u % 4][:, h * 512:(h + 1) * 512], 2)
                    pool.tensor_tensor(p, p, bc(fac[:, (u % 4) * 4 + 2 * h:(u % 4) * 4 + 2 * h + 2], T),
                                       ALU.mult).then_inc(s["scaled_ready"], 1)

            def summed(b, p):
                n = PAIRS * b + p
                pool.wait_ge(s["om_ready"], n + 1 + 1)
                if p == 0:
                    pool.wait_ge(s["out_ps"], b + 1)
                pool.tensor_tensor(o_sum[:, p * T:(p + 1) * T], o_m[:, 0:T], o_m[:, T:2 * T],
                                   ALU.add).then_inc(s["osum_ready"], 1)

            def batch(b, last):
                for sl in range(2, UNITS + 2):
                    if sl > 2 and sl % 2 == 0:
                        summed(b, (sl - 4) // 2)
                    if sl - 1 < UNITS:
                        scaled(b, sl - 1)
                    elif not last and sl == UNITS + 1:
                        scaled(b + 1, 0)
                    if sl == 14 and not last:
                        count = pool.snap(PAIRS * b + PAIRS)
                        pool.wait_ge(s["ident_ready"], 1)
                        pool.wait_ge(s["v_ps"], count)
                        pool.tensor_copy(x_cur[:, :], seq(t_i, b + 1, T)).then_inc(s["xcur_ready"], 1)
                summed(b, PAIRS - 1)

            scaled(0, 0)
            with pool.Fori(0, B - 1) as b:
                batch(b, False)
            batch(B - 1, True)

        @block.scalar
        def _(act):
            act.sem_inc(s["a_gates_act"], 1)
            act.sem_inc(s["b_h2"], 1)
            act.sem_inc(s["g_gT"], 1)
            act.sem_inc(s["pTa_ready"], 1)
            small = [(w_gates[:, :], W), (b_gates[:, :], b4), (b_in[:, :], ib),
                     (scale_bc[:, :], scale.to_broadcast([128, D])), (rw1[:, :], rW1), (rw2[0:R, :], rW2), (rw2[R:2 * R, :], rW2),
                     (rb1_bc[:, :], rb1.to_broadcast([128, R])), (lng_bc[:, :], ln_g.to_broadcast([128, R])),
                     (lnb_bc[:, :], ln_b.to_broadcast([128, R])), (rb2_bc[:, :], rb2.to_broadcast([128, NE])),
                     (q_b[:, :], qb), (k_b[:, :], kb), (ob_w[0:NE, :], ob), (ob_w[32:32 + NE, :], ob)]
            assert len(small) == NSMALL
            for dst, src in small:
                act.dma_start(dst, src).then_inc(s["w_small"], 16)
            act.wait_ge(s["consts"], 2)
            act.wait_ge(s["moment_step"], 6)
            act.activation(rstd[:, :], var, ACT.Ln, bias=eps5[:, 0:1]).then_inc(s["a_ln"], 1)
            act.wait_ge(s["a_ln"], 1)
            act.activation(rstd[:, :], rstd[:, :], ACT.Exp, scale=-0.5).then_inc(s["a_rstd"], 1)
            act.wait_ge(s["w_small"], 16 * NSMALL)
            act.activation(b_ti[:, :], b_in[:, :], ACT.Identity, bias=b_gates[:, 0:1]).then_inc(s["t_e"], 1)
            act.wait_ge(s["t_e"], 1)
            act.mul(b_ti[:, :], b_ti[:, :], 1.0 / CAP).then_inc(s["t_e"], 1)
            act.mul(b_no[:, :], b_gates[:, 2:3], -1.0).then_inc(s["t_e"], 1)
            act.mul(k_b[:, :], k_b[:, :], SCALE).then_inc(s["t_e"], 1)
            act.wait_ge(s["t_e"], 4)
            with act.Fori(0, GROUPS // 2) as i:
                for q in range(2):
                    g = 2 * i + q
                    act.wait_ge(s["a_tp"], g + 1)
                    act.activation(st_b[q][:, :], PS[q][:, :], ACT.Copy).then_inc(s["a_xt"], 1)
                    count = act.snap(4 * g + 2)
                    act.wait_ge(s["ident_ready"], 1)
                    act.wait_ge(s["a_gates_ps"], count)
                    act.activation(seq(t_i, g, GT), ps_s[0][:, 512:1024], ACT.Tanh, bias=b_ti[:, 0:1], scale=1.0 / CAP)
                    count = act.snap(g + 1)
                    act.wait_ge(s["ident_ready"], 1)
                    act.wait_ge(s["a_gates_dve"], count)
                    act.activation(seq(t_a, g, GT), ps_s[0][:, 0:512], ACT.Abs, bias=b_gates[:, 1:2])
                    count = act.snap(4 * g + 3)
                    act.wait_ge(s["ident_ready"], 1)
                    act.wait_ge(s["a_gates_ps"], count)
                    act.activation(seq(t_o, g, GT), ps_s[1][:, 0:512], ACT.Exp, bias=b_no[:, 0:1], scale=-1.0)
                    count = act.snap(4 * g + 4)
                    act.wait_ge(s["ident_ready"], 1)
                    act.wait_ge(s["a_gates_ps"], count)
                    act.activation(seq(t_z, g, GT), ps_s[1][:, 512:1024], ACT.Tanh,
                                   bias=b_gates[:, 3:4]).then_inc(s["a_gates_act"], 1)
            act.wait_ge(s["a_gates_act"], GROUPS + 1)
            act.activation(t_a[:, :], t_a[:, :], ACT.Exp, scale=-1.0).then_inc(s["b_exp"], 1)
            act.wait_ge(s["b_exp"], 1)
            for c in range(4):
                a_c = t_a[:, c * 1024:(c + 1) * 1024]
                act.activation(a_c, a_c, ACT.Ln, bias=1.0).then_inc(s["b_ln"], 1)
            with act.Fori(0, GROUPS) as g:
                count = act.snap(g + 1)
                act.wait_ge(s["ident_ready"], 1)
                act.wait_ge(s["b_d2"], count)
                act.activation(seq(t_f, g, GT), seq(t_f, g, GT), ACT.Exp).then_inc(s["b_fs"], 1)
                count = act.snap(g + 1)
                act.wait_ge(s["ident_ready"], 1)
                act.wait_ge(s["b_d1"], count)
                act.activation(seq(t_i, g, GT), seq(t_i, g, GT), ACT.Exp).then_inc(s["b_is"], 1)
            with act.Fori(0, GROUPS // 2) as i:
                for q in range(2):
                    g = 2 * i + q
                    count = act.snap(g + 1 + 1)
                    act.wait_ge(s["ident_ready"], 1)
                    act.wait_ge(s["b_tp"], count)
                    act.activation(seq(t_f, g, GT), PS[q][:, :], ACT.Copy).then_inc(s["b_h2"], 1)
                    count = act.snap(g + 1 + 1)
                    act.wait_ge(s["ident_ready"], 1)
                    act.wait_ge(s["b_h2"], count)
                    for j in range(4):
                        act.activation(st_b[0][:, j * 128:(j + 1) * 128], t_f[:, bass.ds(g * GT + j * 128, 128)], ACT.Square,
                                       accum_out=ssq[:, bass.ds(4 * g + j, 1)]).then_inc(s["b_sq"], 1)
            act.wait_ge(s["b_sq"], TILES)
            act.activation(ssq[:, :], ssq[:, :], ACT.Ln, bias=eps8[:, 0:1], scale=1.0 / D).then_inc(s["c_ln"], 1)
            act.wait_ge(s["c_ln"], 1)
            act.activation(ssq[:, :], ssq[:, :], ACT.Exp, scale=-0.5).then_inc(s["c_rs"], 1)
            act.wait_ge(s["moment_step"], 12)
            act.activation(rstd[:, :], var, ACT.Ln, bias=eps5[:, 0:1]).then_inc(s["c_ln2"], 1)
            act.wait_ge(s["c_ln2"], 1)
            act.activation(rstd[:, :], rstd[:, :], ACT.Exp, scale=-0.5).then_inc(s["c_rstd"], 1)
            with act.Fori(0, GROUPS // 2) as i:
                for q in range(2):
                    g = 2 * i + q
                    act.wait_ge(s["d_tp"], g + 1 + 1)
                    if q == 0:
                        act.wait_ge(s["d_xt2"], g + 1)
                    else:
                        act.wait_ge(s["d_xt2"], 2 * i + 1)
                    act.activation(st_b[q][:, :], PS[q][:, :], ACT.Copy).then_inc(s["d_xt"], 1)
            act.wait_ge(s["moment_step"], 18)
            act.activation(rstd[:, :], var, ACT.Ln, bias=eps5[:, 0:1]).then_inc(s["e_ln"], 1)
            act.wait_ge(s["e_ln"], 1)
            act.activation(rstd[:, :], rstd[:, :], ACT.Exp, scale=-0.5).then_inc(s["e_rstd"], 1)
            with act.Fori(0, GROUPS // 2) as i:
                for q in range(2):
                    g = 2 * i + q
                    act.wait_ge(s["f_tp"], g + 1 + 1)
                    act.activation(st_b[q][:, 0:2 * 128], PS[q][:, 0:2 * 128], ACT.Relu).then_inc(s["f_hT"], 1)
            act.wait_ge(s["t_step"], TS_DIFF)
            act.activation(gate[:, TILES:2 * TILES], gate[:, TILES:2 * TILES], ACT.Exp).then_inc(s["t_ex"], 1)
            with act.Fori(0, B // 2) as i:
                for q in range(2):
                    b = 2 * i + q
                    count = act.snap(b + 1 + 1)
                    act.wait_ge(s["ident_ready"], 1)
                    act.wait_ge(s["g_tp"], count)
                    act.activation(seq(mask, b, 512), PS[q][:, :], ACT.Copy).then_inc(s["g_mask"], 1)
                    act.activation(sm64[q], PS[2 + q][0:64, 0:128], ACT.Copy).then_inc(s["g_gT"], 1)

            def exps(b, u):
                n = UNITS * b + u
                act.wait_ge(s["negmax_ready"], n + 1)
                for c in range(4):
                    act.activation(prob[u % 4][:, c * T:(c + 1) * T], ps_s[u % 2][:, c * T:(c + 1) * T], ACT.Exp,
                                   bias=negmax[:, (u % 4) * 4 + c:(u % 4) * 4 + c + 1],
                                   accum_out=den[:, (u % 4) * 4 + c:(u % 4) * 4 + c + 1]).then_inc(s["probs_ready"], 1)

            def evac(b, u):
                n = UNITS * b + u
                act.wait_ge(s["pT_ps"], 2 * n + 1)
                act.activation(probT[u % 2][:, 0:512], PS[0][:, :], ACT.Copy).then_inc(s["pTa_ready"], 1)

            def batch(b, last):
                for sl in range(2, UNITS + 2):
                    evac(b, sl - 2)
                    if sl < UNITS:
                        exps(b, sl)
                    elif not last:
                        exps(b + 1, sl - UNITS)

            exps(0, 0)
            exps(0, 1)
            with act.Fori(0, B - 1) as b:
                batch(b, False)
            batch(B - 1, True)

        @block.vector
        def _(dve):
            dve.sem_inc(s["d_hr"], 1)
            dve.sem_inc(s["f_lg"], 1)
            dve.sem_inc(s["g_x1"], 1)
            dve.sem_inc(s["y_ready"], 1)
            dve.sem_inc(s["pTb_ready"], 1)
            dve.sem_inc(s["om_ready"], 1)
            n_stat = [0]

            def bn(tile, src, done):
                dve.bn_stats(stats[:, bass.ds(6 * tile, 6)], src).then_inc(s[done], 1)

            def moments(width):
                def chain(ins):
                    n_stat[0] += 1
                    ins.then_inc(s["moment_step"], 1)
                    dve.wait_ge(s["moment_step"], n_stat[0])
                st = v3(stats[:, :], TILES)
                chain(dve.tensor_tensor(mean, st[:, :, 1], st[:, :, 4], ALU.add))
                chain(dve.tensor_scalar(mean, mean, 0.5, None, ALU.mult))
                chain(dve.tensor_tensor(spread, st[:, :, 1], mean, ALU.subtract))
                chain(dve.tensor_tensor(spread, spread, spread, ALU.mult))
                chain(dve.tensor_tensor(var, st[:, :, 2], st[:, :, 5], ALU.add))
                chain(dve.scalar_tensor_tensor(var, var, 1.0 / width, spread, ALU.mult, ALU.add))

            for c in range(4):
                dve.wait_ge(s[f"x_in{c}"], 16)
                for j in range(8):
                    t = 8 * c + j
                    bn(t, xs[:, t * D:(t + 1) * D], "a_stats")
            dve.wait_ge(s["a_stats"], TILES)
            moments(D)
            dve.wait_ge(s["a_rstd"], 1)
            with dve.Fori(0, GROUPS // 2) as i:
                for q in range(2):
                    g = 2 * i + q
                    for j in range(4):
                        t = 4 * g + j
                        dve.tensor_scalar(st_a[q][:, j * 128:(j + 1) * 128], xs[:, bass.ds(t * D, D)],
                                          mean[:, bass.ds(t, 1)], rstd[:, bass.ds(t, 1)],
                                          ALU.subtract, ALU.mult).then_inc(s["a_xn"], 1)
                    dve.wait_ge(s["a_gates_ps"], 4 * g + 1)
                    dve.tensor_scalar(seq(t_f, g, GT), ps_s[0][:, 0:512], b_gates[:, 1:2], 0.0,
                                      ALU.add, ALU.max).then_inc(s["a_gates_dve"], 1)

            with dve.Fori(0, GROUPS) as g:
                f_g, a_g, i_g, z_g, o_g = (seq(t, g, GT) for t in (t_f, t_a, t_i, t_z, t_o))
                dve.wait_ge(s["b_ln"], 4)
                dve.scalar_tensor_tensor(f_g, f_g, -1.0, a_g, ALU.mult, ALU.subtract).then_inc(s["b_f"], 1)
                dve.wait_ge(s["b_f"], g + 1)
                dve.wait_ge(s["b_i"], g + 1)
                dve.wait_ge(s["consts"], 12)

                def part(tab, w, k, off=0):
                    return tab[:, bass.ds(g * 2 * w + k * w + off, T)]
                for k in range(2):
                    dve.tensor_tensor_scan(part(t_m, T + 1, k, 1), part(t_f, T, k), part(t_i, T, k), 0.0,
                                           ALU.add, ALU.max).then_inc(s["b_m"], 1)
                dve.wait_ge(s["b_is"], g + 1)
                dve.wait_ge(s["b_fs"], g + 1)
                for k in range(2):
                    dve.tensor_tensor_scan(part(t_a, T, k), part(t_f, T, k), part(t_i, T, k), 0.0,
                                           ALU.mult, ALU.add).then_inc(s["b_n"], 1)
                dve.wait_ge(s["b_u"], g + 1)
                for k in range(2):
                    dve.tensor_tensor_scan(part(t_m, T + 1, k, 1), part(t_f, T, k), part(t_z, T, k), 0.0,
                                           ALU.mult, ALU.add).then_inc(s["b_c"], 1)
                dve.wait_ge(s["b_n"], 2 * g + 2)
                dve.tensor_scalar(a_g, a_g, 1e-6, None, ALU.add).then_inc(s["b_ne"], 1)
                dve.wait_ge(s["b_ne"], g + 1)
                dve.scalar_tensor_tensor(a_g, o_g, 1.0, a_g, ALU.add, ALU.mult).then_inc(s["b_d"], 1)
                count = dve.snap(g + 1)
                dve.wait_ge(s["ident_ready"], 1)
                dve.wait_ge(s["b_d"], count)
                dve.reciprocal(a_g, a_g).then_inc(s["b_r"], 1)

            with dve.Fori(0, GROUPS // 2) as i:
                for q in range(2):
                    g = 2 * i + q
                    dve.wait_ge(s["b_r"], GROUPS)
                    dve.wait_ge(s["b_c"], 2 * GROUPS)
                    if q == 0:
                        dve.wait_ge(s["b_tp"], 2 * i + 1)
                    m = t_m[:, bass.ds(g * 2 * (T + 1), 2 * (T + 1))].rearrange("p (b t) -> p b t", b=2)
                    dve.tensor_tensor(v3(st_a[q][:, :], 2), v3(seq(t_a, g, GT), 2), m[:, :, 1:T + 1],
                                      ALU.mult).then_inc(s["b_h"], 1)
            dve.wait_ge(s["c_rs"], 1)
            with dve.Fori(0, GROUPS) as g:
                for j in range(4):
                    t = 4 * g + j
                    h_t = t_f[:, bass.ds(t * D, D)]
                    dve.scalar_tensor_tensor(h_t, h_t, ssq[:, bass.ds(t, 1)], scale_bc[:, :],
                                             ALU.mult, ALU.mult).then_inc(s["c_h3"], 1)
                dve.wait_ge(s["c_h3"], 4 * g + 4)
                dve.tensor_tensor(seq(xs, g, GT), seq(xs, g, GT), seq(t_f, g, GT), ALU.add).then_inc(s["c_x1"], 1)
                dve.wait_ge(s["c_x1"], g + 1)
                for j in range(4):
                    t = 4 * g + j
                    bn(t, xs[:, bass.ds(t * D, D)], "c_stats")
            dve.wait_ge(s["c_stats"], TILES)
            moments(D)
            dve.wait_ge(s["c_rstd"], 1)
            with dve.Fori(0, GROUPS // 2) as i:
                for q in range(2):
                    g = 2 * i + q
                    if q == 0:
                        dve.wait_ge(s["d_tp"], 2 * i + 1)
                    for j in range(4):
                        t = 4 * g + j
                        dve.tensor_scalar(st_a[q][:, j * 128:(j + 1) * 128], xs[:, bass.ds(t * D, D)],
                                          mean[:, bass.ds(t, 1)], rstd[:, bass.ds(t, 1)],
                                          ALU.subtract, ALU.mult).then_inc(s["d_xn"], 1)
                    dve.wait_ge(s["d_hr_ps"], g + 1)
                    dve.tensor_tensor(v3(seq(hr, g, 4 * R), 4), v3(PS[2][:, 0:4 * R], 4),
                                      rb1_bc[:, :].rearrange("p (o r) -> p o r", o=1).to_broadcast([128, 4, R]),
                                      ALU.add).then_inc(s["d_hr"], 1)
            dve.wait_ge(s["d_hr"], GROUPS + 1)
            with dve.Fori(0, GROUPS) as g:
                for j in range(4):
                    t = 4 * g + j
                    bn(t, hr[:, bass.ds(t * R, R)], "e_stats")
            dve.wait_ge(s["e_stats"], TILES)
            moments(R)
            dve.wait_ge(s["e_rstd"], 1)
            with dve.Fori(0, GROUPS) as g:
                for j in range(4):
                    t = 4 * g + j
                    dve.tensor_scalar(hr[:, bass.ds(t * R, R)], hr[:, bass.ds(t * R, R)],
                                      mean[:, bass.ds(t, 1)], rstd[:, bass.ds(t, 1)],
                                      ALU.subtract, ALU.mult).then_inc(s["e_n"], 1)
            with dve.Fori(0, GROUPS // 2) as i:
                for q in range(2):
                    g = 2 * i + q
                    if q == 0:
                        dve.wait_ge(s["f_tp"], 2 * i + 1)
                    dve.wait_ge(s["e_b"], g + 1)
                    dve.tensor_copy(st_a[q][:, 0:4 * R], seq(hr, g, 4 * R)).then_inc(s["f_st"], 1)
                    dve.wait_ge(s["f_lg_ps"], g + 1)
                    lg4 = seq(lg, g, 4 * NE).rearrange("p (a k e) -> p a k e", a=2, k=2)
                    for k in range(2):
                        ps4 = PS[2 + k][:, 0:4 * NE].rearrange("p (a k e) -> p a k e", a=2, k=2)
                        last = dve.tensor_tensor(lg4[:, :, k, :], ps4[:, :, k, :],
                                                 rb2_bc[:, :].rearrange("p (o r) -> p o r", o=1).to_broadcast([128, 2, NE]),
                                                 ALU.add)
                    last.then_inc(s["f_lg"], 1)
            n_step = [0]

            def step(ins):
                n_step[0] += 1
                ins.then_inc(s["t_step"], 1)
                dve.wait_ge(s["t_step"], n_step[0])
                return n_step[0]

            dve.wait_ge(s["f_lg"], GROUPS + 1)
            lg3 = v3(lg[:, :], TILES)
            oh4 = oh[:, :].rearrange("p (t r e) -> p t r e", t=TILES, r=2)
            tmp3 = v3(st_a[0][:, 0:TILES * NE], TILES)
            best = [gate[:, 0:TILES], gate[:, TILES:2 * TILES]]
            hit = ssq[:, :]
            rev3 = rev[:, :].rearrange("p (o e) -> p o e", o=1).to_broadcast([128, TILES, NE])
            for r in range(2):
                step(dve.tensor_reduce(best[r], lg3, AX.X, ALU.max))
                step(dve.tensor_tensor(tmp3, lg3, bc(best[r], NE), ALU.is_equal))
                step(dve.tensor_tensor(tmp3, tmp3, rev3, ALU.mult))
                step(dve.tensor_reduce(hit, tmp3, AX.X, ALU.max))
                step(dve.tensor_tensor(oh4[:, :, r, :], tmp3, bc(hit, NE), ALU.is_equal))
                if r == 0:
                    step(dve.scalar_tensor_tensor(lg3, oh4[:, :, 0, :], BELOW, lg3, ALU.mult, ALU.add))
            k = step(dve.tensor_tensor(best[1], best[1], best[0], ALU.subtract))
            assert k == TS_DIFF
            dve.wait_ge(s["t_ex"], 1)
            step(dve.tensor_scalar(best[0], best[1], 1.0, None, ALU.add))
            step(dve.reciprocal(best[0], best[0]))
            step(dve.tensor_tensor(best[1], best[1], best[0], ALU.mult))
            g83 = v3(g8[:, :], TILES)[:, :, 0:NE]
            step(dve.tensor_tensor(tmp3, oh4[:, :, 0, :], bc(best[0], NE), ALU.mult))
            step(dve.tensor_tensor(g83, oh4[:, :, 1, :], bc(best[1], NE), ALU.mult))
            dve.wait_ge(s["consts"], 13)
            step(dve.tensor_tensor(g83, g83, tmp3, ALU.add))
            with dve.Fori(0, B // 2) as i:
                for q in range(2):
                    b = 2 * i + q
                    if q == 0:
                        dve.wait_ge(s["g_tp"], 2 * i + 1)
                    for r in range(2):
                        for half in range(2):
                            src = oh[:, bass.ds(4 * NE * b + (2 * half + r) * NE, NE)]
                            src = src.rearrange("p (o e f) -> p o e f", o=1, f=1).to_broadcast([128, 2, NE, DH])
                            c = 2 * r + half
                            dst = st_a[q][:, c * 128:(c + 1) * 128].rearrange("p (h e d) -> p h e d", h=2, e=NE)
                            last = dve.tensor_copy(dst, src)
                    last.then_inc(s["g_st"], 1)
                    dve.tensor_copy(g_st[q], seq(g8, b, 64)).then_inc(s["g_st"], 1)
                    dve.wait_ge(s["g_ob_ps"], b + 1)
                    x_b = seq(xs, b, 2 * D)
                    dve.tensor_tensor(v3(x_b, 2), v3(x_b, 2), v3(ps_s[q][:, :], 2)[:, :, 0:D], ALU.add).then_inc(s["g_x1"], 1)

            dve.wait_ge(s["g_mask"], B)

            def qk_evac(b, p):
                n = PAIRS * b + p
                dve.wait_ge(s["qk_ps"], n + 1)
                m = v3(seq(mask, b, 512), 2)
                qp = PS[3][:, 0:T].rearrange("p (o t) -> p o t", o=1).to_broadcast([128, 2, T])
                dve.scalar_tensor_tensor(v3(q_m[p % 2][:, :], 2), qp, q_b[:, p:p + 1], m,
                                         ALU.add, ALU.mult).then_inc(s["q_ready"], 1)
                dve.tensor_scalar(k_m[p % 2][:, :], PS[3][:, T:2 * T], SCALE, k_b[:, p:p + 1],
                                  ALU.mult, ALU.add).then_inc(s["k_ready"], 1)

            def v_evac(b, p):
                n = PAIRS * b + p
                dve.wait_ge(s["v_ps"], n + 1)
                dve.tensor_tensor(v3(v_m[p % 4][:, :], 2), v3(PS[3][:, 0:2 * 128], 2),
                                  v_b[:, p * 128:(p + 1) * 128].rearrange("p (o c) -> p o c", o=1).to_broadcast([128, 2, 128]),
                                  ALU.add).then_inc(s["v_ready"], 1)

            def maxes(b, u):
                n = UNITS * b + u
                dve.wait_ge(s["scores_ready"], n + 1)
                dve.tensor_reduce(negmax[:, (u % 4) * 4:(u % 4) * 4 + 4], v3(ps_s[u % 2][:, :], 4), AX.X, ALU.max,
                                  negate=True).then_inc(s["negmax_ready"], 1)

            def factors(b, u):
                n = UNITS * b + u
                f = fac[:, (u % 4) * 4:(u % 4) * 4 + 4]
                dve.wait_ge(s["probs_ready"], 4 * n + 4)
                dve.reciprocal(f, den[:, (u % 4) * 4:(u % 4) * 4 + 4]).then_inc(s["rden_ready"], 1)
                dve.wait_ge(s["rden_ready"], n + 1)
                r = u % 2
                g2 = gate[:, bass.ds(r * TILES + 2 * b, 2)].rearrange("p (o t) -> p o t", o=1).to_broadcast([128, 2, 2])
                dve.tensor_tensor(v3(f, 2), v3(f, 2), g2, ALU.mult).then_inc(s["fac_ready"], 1)

            def evac(b, u):
                n = UNITS * b + u
                dve.wait_ge(s["pT_ps"], 2 * n + 2)
                dve.tensor_copy(probT[u % 2][:, 512:1024], PS[1][:, :]).then_inc(s["pTb_ready"], 1)

            def masked(b, p):
                n = PAIRS * b + p
                dve.wait_ge(s["pv_ps"], 2 * n + 2)
                dve.wait_ge(s["osum_ready"], n + 1)
                dve.tensor_tensor(o_m, PS[2][:, :], seq(mask, b, 512), ALU.mult).then_inc(s["om_ready"], 1)

            def batch(b, last):
                for sl in range(2, UNITS + 2):
                    nb, u = (b, sl) if sl < UNITS else (b + 1, sl - UNITS)
                    fb, fu = (b, sl - 1) if sl - 1 < UNITS else (b + 1, sl - 1 - UNITS)
                    if fb is b or not last:
                        factors(fb, fu)
                    if nb is b or not last:
                        maxes(nb, u)
                    evac(b, sl - 2)
                    p = sl // 2 + 1
                    pb, p = (b, p) if p < PAIRS else (b + 1, p - PAIRS)
                    if pb is b or not last:
                        (qk_evac if sl % 2 == 0 else v_evac)(pb, p)
                    if sl % 2 == 1:
                        masked(b, (sl - 2) // 2)
                dve.wait_ge(s["out_ps"], b + 1 + 1)
                x_b = seq(xs, b, 2 * D)
                dve.tensor_tensor(x_b, PS[3][:, 0:2 * D], x_b, ALU.add).then_inc(s["y_ready"], 1)

            dve.wait_ge(s["w_in"], 16 * 5)
            qk_evac(0, 0)
            v_evac(0, 0)
            maxes(0, 0)
            qk_evac(0, 1)
            factors(0, 0)
            maxes(0, 1)
            v_evac(0, 1)
            with dve.Fori(0, B - 1) as b:
                batch(b, False)
            batch(B - 1, True)

        @block.tensor
        def _(pe):
            pe.sem_inc(s["b_tp"], 1)
            pe.sem_inc(s["d_tp"], 1)
            pe.sem_inc(s["f_tp"], 1)
            pe.sem_inc(s["g_tp"], 1)
            pe.sem_inc(s["out_ps"], 1)
            def transposes(dst, src, done, width=128):
                for j in range(4):
                    last = pe.transpose(dst[0:width, j * 128:(j + 1) * 128], src[:, j * width:(j + 1) * width], ident[:, :])
                last.then_inc(s[done], 1)

            pe.wait_ge(s["ident_ready"], 1)
            pe.wait_ge(s["w_small"], 16 * NSMALL)
            pg = [ps_s[0][:, 0:512], ps_s[0][:, 512:1024], ps_s[1][:, 0:512], ps_s[1][:, 512:1024]]
            with pe.Fori(0, GROUPS // 2) as i:
                for q in range(2):
                    g = 2 * i + q
                    pe.wait_ge(s["a_xn"], 4 * g + 4)
                    transposes(PS[q], st_a[q], "a_tp")
                    pe.wait_ge(s["a_xt"], g + 1)
                    for k, w in enumerate((1, 0, 2, 3)):
                        if k == 0:
                            pe.wait_ge(s["a_gates_act"], g + 1)
                        pe.matmul(pg[k], w_gates[:, w * D:(w + 1) * D], st_b[q][:, :], start=True,
                                  stop=True).then_inc(s["a_gates_ps"], 1)
            with pe.Fori(0, GROUPS // 2) as i:
                for q in range(2):
                    g = 2 * i + q
                    pe.wait_ge(s["b_h"], g + 1)
                    if q == 0:
                        pe.wait_ge(s["b_h2"], 2 * i + 1)
                    transposes(PS[q], st_a[q], "b_tp")
            with pe.Fori(0, GROUPS // 2) as i:
                for q in range(2):
                    g = 2 * i + q
                    pe.wait_ge(s["d_xn"], 4 * g + 4)
                    if q == 0:
                        pe.wait_ge(s["b_sq"], TILES)
                    transposes(PS[q], st_a[q], "d_tp")
                    pe.wait_ge(s["d_xt"], g + 1)
                    pe.wait_ge(s["d_hr"], g + 1)
                    for j in range(4):
                        last = pe.matmul(PS[2][:, j * R:(j + 1) * R], st_b[q][:, j * 128:(j + 1) * 128], rw1[:, :],
                                         start=True, stop=True)
                    last.then_inc(s["d_hr_ps"], 1)
            with pe.Fori(0, GROUPS // 2) as i:
                for q in range(2):
                    g = 2 * i + q
                    pe.wait_ge(s["f_st"], g + 1)
                    for m in range(2):
                        last = pe.transpose(PS[q][:, m * 128:(m + 1) * 128], st_a[q][:, m * 128:(m + 1) * 128], ident[:, :])
                    last.then_inc(s["f_tp"], 1)
                    pe.wait_ge(s["f_hT"], g + 1)
                    pe.wait_ge(s["f_lg"], g + 1)
                    for j in range(4):
                        k = 64 * (j % 2)
                        last = pe.matmul(PS[2 + j % 2][:, j * NE:(j + 1) * NE],
                                         st_b[q][k:k + R, j // 2 * 128:(j // 2 + 1) * 128],
                                         rw2[k:k + R, :], start=True, stop=True)
                    last.then_inc(s["f_lg_ps"], 1)
            with pe.Fori(0, B // 2) as i:
                for q in range(2):
                    b = 2 * i + q
                    pe.wait_ge(s["g_st"], 2 * b + 2)
                    if q == 0:
                        pe.wait_ge(s["g_gT"], 2 * i + 1)
                    for j in range(4):
                        pe.transpose(PS[q][:, j * 128:(j + 1) * 128], st_a[q][:, j * 128:(j + 1) * 128], ident[:, :])
                    pe.transpose(PS[2 + q][0:64, 0:128], g_st[q], ident[:, :]).then_inc(s["g_tp"], 1)
                    pe.wait_ge(s["g_gT"], b + 1 + 1)
                    if q == 0:
                        pe.wait_ge(s["g_x1"], 2 * i + 1)
                    for half in range(2):
                        last = pe.matmul(ps_s[q][:, half * 512:half * 512 + 128], sm64[q][32 * half:32 * half + NE, :],
                                         ob_w[32 * half:32 * half + NE, :], start=True, stop=True)
                    last.then_inc(s["g_ob_ps"], 1)

            def qk_proj(b, p):
                n = PAIRS * b + p
                if p == 0:
                    pe.wait_ge(s["xcur_ready"], b + 1)
                if not (isinstance(b, int) and n == 0):
                    pe.wait_ge(s["v_ready"], n)
                if p == 2:
                    pe.wait_ge(s["y_ready"], b + 1)
                pe.matmul(PS[3][:, 0:T], q_w[:, p * 128:(p + 1) * 128], x_cur[:, :], start=True, stop=True)
                pe.matmul(PS[3][:, T:2 * T], k_w[:, p * 128:(p + 1) * 128], x_cur[:, :], start=True,
                          stop=True).then_inc(s["qk_ps"], 1)

            def v_proj(b, p):
                n = PAIRS * b + p
                pe.wait_ge(s["k_ready"], n + 1)
                for c in range(2):
                    last = pe.matmul(PS[3][:, c * 128:(c + 1) * 128], x_cur[:, c * 128:(c + 1) * 128],
                                     v_w[:, p * 128:(p + 1) * 128], start=True, stop=True)
                last.then_inc(s["v_ps"], 1)

            def scores(b, u):
                n = UNITS * b + u
                p, r = u // 2, u % 2
                pe.wait_ge(s["k_ready"], PAIRS * b + p + 1)
                if not (isinstance(b, int) and n < 2):
                    pe.wait_ge(s["probs_ready"], 4 * (n - 1))
                for j in range(2):
                    for h in range(2):
                        last = pe.matmul(ps_s[u % 2][:, h * 512 + j * T:h * 512 + (j + 1) * T],
                                         q_m[p % 2][64 * h:64 * h + 64, r * T + j * 128:r * T + (j + 1) * 128],
                                         k_m[p % 2][64 * h:64 * h + 64, :], start=True, stop=True)
                last.then_inc(s["scores_ready"], 1)

            def to_keys(b, u):
                n = UNITS * b + u
                for h in range(2):
                    pe.wait_ge(s["scaled_ready"], 2 * n + 1 + h)
                    pe.wait_ge(s[("pTa_ready", "pTb_ready")[h]], n + 1)
                    for j in range(2):
                        for c in range(2):
                            last = pe.transpose(PS[h][:, c * T + j * 128:c * T + (j + 1) * 128],
                                                prob[u % 4][:, h * 512 + j * T + c * 128:h * 512 + j * T + (c + 1) * 128],
                                                ident[:, :])
                    last.then_inc(s["pT_ps"], 1)

            def values(b, u):
                n = UNITS * b + u
                p, r = u // 2, u % 2
                pe.wait_ge(s["pTa_ready"], n + 1 + 1)
                pe.wait_ge(s["pTb_ready"], n + 1 + 1)
                if r == 0:
                    pe.wait_ge(s["v_ready"], PAIRS * b + p + 1)
                    pe.wait_ge(s["om_ready"], PAIRS * b + p + 1)
                for c in range(2):
                    for h in range(2):
                        last = pe.matmul(PS[2][64 * h:64 * h + 64, r * T:(r + 1) * T],
                                         v_m[p % 4][:, c * 128 + 64 * h:c * 128 + 64 * h + 64],
                                         probT[u % 2][:, h * 512 + c * T:h * 512 + (c + 1) * T],
                                         start=(c == 0), stop=(c == 1))
                last.then_inc(s["pv_ps"], 1)

            def project(b):
                pe.wait_ge(s["v_ready"], PAIRS * b + PAIRS)
                for p in range(PAIRS):
                    if p == PAIRS - 1 or p == 0:
                        pe.wait_ge(s["osum_ready"], (PAIRS * b + (PAIRS if p else PAIRS - 1)) + 1)
                    for half in range(2):
                        last = pe.matmul(PS[3][:, half * 128:(half + 1) * 128],
                                         o_sum[:, p * T + half * 128:p * T + (half + 1) * 128],
                                         o_w[:, p * D:(p + 1) * D], start=(p == 0 and half == 0),
                                         stop=(p == PAIRS - 1), skip_group_check=True)
                last.then_inc(s["out_ps"], 1)

            def batch(b, last):
                for sl in range(2, UNITS + 2):
                    nb, u = (b, sl) if sl < UNITS else (b + 1, sl - UNITS)
                    if nb is b or not last:
                        scores(nb, u)
                    to_keys(b, sl - 2)
                    p = sl // 2 + 1
                    pb, p = (b, p) if p < PAIRS else (b + 1, p - PAIRS)
                    if pb is b or not last:
                        (qk_proj if sl % 2 == 0 else v_proj)(pb, p)
                    values(b, sl - 2)
                if not last:
                    pe.wait_ge(s["v_ready"], PAIRS * (b + 1) + 2)
                project(b)

            pe.wait_ge(s["w_in"], 16 * 5)
            pe.wait_ge(s["g_mask"], B)
            qk_proj(0, 0)
            v_proj(0, 0)
            scores(0, 0)
            qk_proj(0, 1)
            scores(0, 1)
            v_proj(0, 1)
            with pe.Fori(0, B - 1) as b:
                batch(b, False)
            batch(B - 1, True)


NSMALL = 15
TS_DIFF = 12


def kernel(**inputs):
    import numpy as np
    import concourse.bacc as bacc
    from concourse.bass_utils import run_bass_kernel_spmd
    a = {k.replace("L0_attn_", "a_").replace("L0_ffn_", "f_"): np.asarray(v) for k, v in inputs.items()}

    def by_head(w):
        return w.reshape(NE, H, DH, D).transpose(3, 1, 0, 2).reshape(D, H * NE * DH)

    def by_pair(v):
        return v.reshape(NE, PAIRS, 2, DH).transpose(2, 0, 3, 1).reshape(2 * NE * DH, PAIRS)

    arrays = {
        "x": a["a_x"], "W": a["a_W"], "b4": a["a_b"].reshape(4, D).T, "ib": a["a_input_bias"].reshape(D, 1),
        "scale": a["a_scale"].reshape(1, D), "rW1": a["f_rW1"].T, "rb1": a["f_rb1"].reshape(1, R),
        "ln_g": a["f_ln_g"].reshape(1, R), "ln_b": a["f_ln_b"].reshape(1, R), "rW2": a["f_rW2"].T,
        "rb2": a["f_rb2"].reshape(1, NE),
        "qW": by_head(a["f_qW"]), "qb": by_pair(a["f_qb"]), "kW": by_head(a["f_kW"]), "kb": by_pair(a["f_kb"]),
        "vW": by_head(a["f_vW"]), "vb": a["f_vb"].reshape(NE, H, DH).transpose(1, 0, 2).reshape(1, H * NE * DH),
        "oW": a["f_oW"].reshape(NE, D, PAIRS, 2, DH).transpose(3, 0, 4, 2, 1).reshape(2 * NE * DH, PAIRS * D),
        "ob": a["f_ob"],
    }
    arrays = {k: np.ascontiguousarray(v) for k, v in arrays.items()}
    nc = bacc.Bacc("TRN2", target_bir_lowering=False, num_devices=1)
    args = [nc.dram_tensor("in_" + k, v.shape, mybir.dt.from_np(v.dtype), kind="ExternalInput").ap()
            for k, v in arrays.items()]
    out = nc.dram_tensor("out_0", (B, T, D), fp32, kind="ExternalOutput").ap()
    xlstm_moe_attention(nc, *args, out)
    r = run_bass_kernel_spmd(nc, [{"in_" + k: v for k, v in arrays.items()}], core_ids=[0])
    return r.results[0]["out_0"]
```

```python
import concourse.bass as bass
from concourse import mybir
from contextlib import ExitStack

fp32 = mybir.dt.float32
bf16 = mybir.dt.bfloat16
ALU = mybir.AluOpType
ACT = mybir.ActivationFunctionType
AX = mybir.AxisListType

B, T, D = 16, 256, 128
TILES = B * T // 128
NE, H, DH = 8, 16, 8
R = D // 2
PAIRS = H // 2
UNITS = 2 * PAIRS
CAP = 10.0
SCALE = float(DH) ** -0.5
BELOW = -3.0e38
NSMALL = 11
TOP_STEPS = 16


def xlstm_moe_attention(nc, x, W, b4, ib, scale, rW1, rb1, ln_g, ln_b, rW2, rb2,
                        qW, qb, kW, kb, vW, vb, oW, ob, out):
    ctx = ExitStack()
    with ctx:
        def sb(name, shape, dt=fp32):
            return ctx.enter_context(nc.sbuf_tensor(name, shape, dt))

        def ps(name, shape):
            return ctx.enter_context(nc.psum_tensor(name, shape, fp32))

        def sem(name):
            return ctx.enter_context(nc.semaphore(name))

        w_gates = sb("w_gates", [128, 4 * D])
        b_gates = sb("b_gates", [128, 4])
        b_in = sb("b_in", [128, 1])
        b_ti = sb("b_ti", [128, 1])
        b_no = sb("b_no", [128, 1])
        scale_bc = sb("scale_bc", [128, D])
        rw1 = sb("rw1", [128, R])
        rw2 = sb("rw2", [2 * R, 2 * NE])
        rb1_bc = sb("rb1_bc", [128, R])
        lng_bc = sb("lng_bc", [128, R])
        lnb_bc = sb("lnb_bc", [128, R])
        rb2_bc = sb("rb2_bc", [128, NE])
        q_w = sb("q_w", [128, H * NE * DH])
        k_w = sb("k_w", [128, H * NE * DH])
        v_w = sb("v_w", [128, H * NE * DH])
        o_w = sb("o_w", [128, PAIRS * D])
        q_b = sb("q_b", [128, PAIRS])
        k_b = sb("k_b", [128, PAIRS])
        v_b = sb("v_b", [128, H * NE * DH])
        ob_w = sb("ob_w", [NE, D])
        ident = sb("ident", [128, 128])
        rev = sb("rev", [128, NE])
        cap = sb("cap", [128, 1])
        mhalf = sb("mhalf", [128, 2])
        fence = sb("fence", [128, 1])

        xs = sb("xs", [128, TILES * D])
        gate = sb("gate", [128, 2 * TILES])
        mask = sb("mask", [128, B * 2 * T], bf16)

        st1 = sb("st1", [128, 12])
        mv1 = sb("mv1", [128, 4])
        ve1 = sb("ve1", [128, 2])
        rs1 = sb("rs1", [128, 2])
        x_n = sb("x_n", [128, T])
        x_nT = sb("x_nT", [128, T])
        g_r = sb("g_r", [128, T])
        g_a = sb("g_a", [128, T])
        g_i = sb("g_i", [128, T])
        g_o = sb("g_o", [128, T])
        g_z = sb("g_z", [128, T])
        run_m = sb("run_m", [128, T + 1])
        d_f = sb("d_f", [128, T])
        d_i = sb("d_i", [128, T])
        s_f = sb("s_f", [128, T])
        s_i = sb("s_i", [128, T])
        i_z = sb("i_z", [128, T])
        run_n = sb("run_n", [128, T])
        run_c = sb("run_c", [128, T])
        dn = sb("dn", [128, T])
        rdn = sb("rdn", [128, T])
        hid = sb("hid", [128, T])

        h_tok = sb("h_tok", [128, T])
        sq = sb("sq", [128, T])
        ssq = sb("ssq", [128, 2])
        ms = sb("ms", [128, 2])
        rms = sb("rms", [128, 2])
        st2 = sb("st2", [128, 12])
        mv2 = sb("mv2", [128, 4])
        ve2 = sb("ve2", [128, 2])
        rs2 = sb("rs2", [128, 2])
        x_n2 = sb("x_n2", [128, T])
        x_hT = sb("x_hT", [128, T])
        hr = sb("hr", [128, 2 * R])
        st3 = sb("st3", [128, 12])
        mv3 = sb("mv3", [128, 4])
        ve3 = sb("ve3", [128, 2])
        rs3 = sb("rs3", [128, 2])
        hr_n = sb("hr_n", [128, 2 * R])
        hr_g = sb("hr_g", [128, 2 * R])
        hr_b = sb("hr_b", [128, 2 * R])
        hr_T = sb("hr_T", [128, 128])
        lg = sb("lg", [128, 2 * NE])
        best = sb("best", [128, 4])
        eq = sb("eq", [128, 2 * NE])
        hit = sb("hit", [128, 2])
        oh = sb("oh", [128, 4 * NE])
        diff = sb("diff", [128, 2])
        ediff = sb("ediff", [128, 2])
        gsum = sb("gsum", [128, 2])
        g_e = sb("g_e", [128, 2 * 2 * NE])
        oh_w = sb("oh_w", [128, 4 * 128])
        g_w = sb("g_w", [128, 2 * 128])
        g_T = sb("g_T", [NE, T])

        x_cur = sb("x_cur", [128, T])
        q_m = [sb(f"q_m{i}", [128, 2 * T]) for i in range(2)]
        k_m = [sb(f"k_m{i}", [128, T]) for i in range(2)]
        v_m = [sb(f"v_m{i}", [128, 2 * 128]) for i in range(4)]
        prob = [sb(f"prob{i}", [128, 1024]) for i in range(4)]
        probT = [sb(f"probT{i}", [128, 1024]) for i in range(2)]
        negmax = sb("negmax", [128, 4 * 4])
        den = sb("den", [128, 4 * 4])
        fac = sb("fac", [128, 4 * 4])
        o_m = sb("o_m", [128, 2 * T])
        o_sum = sb("o_sum", [128, PAIRS * T])

        ps_s = [ps(f"ps_s{i}", [128, 1024]) for i in range(2)]
        ps_t = [ps(f"ps_t{i}", [128, 512]) for i in range(2)]
        ps_v = ps("ps_v", [128, 512])
        ps_m = ps("ps_m", [128, 512])

        names = """x_in x_first w_in w_first w_small kb_ready zero ident_ready consts b_ready tail_zero
        stats1 mv1_ready ve1_ready rs1_ready xn_ready xn_ps xnT_ready fi_ps a_ready fi_ready oz_ps oz_ready
        i_ready ea_ready ln_ready f_ready m_ready df_sum df_ready di_ready sf_ready si_ready iz_ready n_ready c_ready
        ne_ready dn_ready rdn_ready h_ready
        h_ps ssq_ready htok_ready ms_ready rms_ready h3_ready x1_ready stats2 mv2_ready ve2_ready rs2_ready xn2_ready
        xn2_ps xhT_ready hr_ps hr_ready stats3 mv3_ready ve3_ready rs3_ready hrn_ready hrg_ready hrb_ready
        hrT_ps hrT_ready lg_ps lg_ready top diff_ready ediff_ready ohw_ready gw_ready mask_ps mask_ready gT_ps gT_ready
        ob_ps ob_ready
        xcur_ready qk_ps k_ready v_ps v_ready scores_ready negmax_ready probs_ready rden_ready fac_ready
        scaled_ready pT_ps pT_ready pv_ps om_ready osum_ready out_ps y_ready y_out""".split()
        s = {n: sem(n) for n in names}
        block = ctx.enter_context(nc.Block())

        def seq(tab, g, per):
            return tab[:, bass.ds(g * per, per)]

        def bc(ap, n):
            return ap.rearrange("p (a o) -> p a o", o=1).to_broadcast([ap.shape[0], ap.shape[1], n])

        def tile2(ap):
            return ap.rearrange("p (a b) -> p a b", a=2)

        def over_tiles(ap):
            return ap.rearrange("p (o r) -> p o r", o=1).to_broadcast([128, 2, ap.shape[1]])

        def later(q):
            return not (isinstance(q, int) and q == 0)


        @block.sync
        def _(sp):
            xv = x.rearrange("b (h p) d -> p (b h) d", p=128)
            sp.dma_start(xs[:, 0:4 * D].rearrange("p (a d) -> p a d", a=4), xv[:, 0:4, :]).then_inc(s["x_first"], 16)
            small = [(scale_bc[:, :], scale.to_broadcast([128, D])), (rw1[:, :], rW1),
                     (rb1_bc[:, :], rb1.to_broadcast([128, R])), (lng_bc[:, :], ln_g.to_broadcast([128, R])),
                     (lnb_bc[:, :], ln_b.to_broadcast([128, R])), (rb2_bc[:, :], rb2.to_broadcast([128, NE])),
                     (q_b[:, :], qb), (k_b[:, :], kb), (ob_w[:, :], ob)]
            assert len(small) + 2 == NSMALL
            for dst, src in small:
                sp.dma_start(dst, src).then_inc(s["w_small"], 16)
            sp.wait_ge(s["tail_zero"], 1)
            sp.dma_start(rw2[0:R, 0:NE], rW2).then_inc(s["w_small"], 16)
            sp.dma_start(rw2[R:2 * R, NE:2 * NE], rW2).then_inc(s["w_small"], 16)
            sp.dma_start(q_w[:, :], qW).then_inc(s["w_in"], 16)
            sp.dma_start(k_w[:, :], kW).then_inc(s["w_in"], 16)
            sp.dma_start(v_w[:, :], vW).then_inc(s["w_in"], 16)
            sp.dma_start(v_b[:, :], vb.to_broadcast([128, H * NE * DH])).then_inc(s["w_in"], 16)
            sp.dma_start(o_w[:, :], oW).then_inc(s["w_in"], 16)
            sp.dma_start(xs[:, 4 * D:16 * D].rearrange("p (a d) -> p a d", a=12), xv[:, 4:16, :]).then_inc(s["x_in"], 16)
            sp.dma_start(xs[:, 16 * D:].rearrange("p (a d) -> p a d", a=TILES - 16), xv[:, 16:, :]).then_inc(s["x_in"], 16)
            yv = out.rearrange("b (h p) d -> p (b h) d", p=128)
            with sp.Fori(0, B) as b:
                sp.wait_ge(s["y_ready"], b + 2)
                sp.dma_start(yv[:, bass.ds(2 * b, 2), :], tile2(seq(xs, b, 2 * D))).then_inc(s["y_out"], 16)
            sp.wait_ge(s["y_out"], 16 * B)

        @block.gpsimd
        def _(pool):
            pool.sem_inc(s["osum_ready"], 1)
            pool.memset(ident[:, :], 0.0).then_inc(s["zero"], 1)
            pool.wait_ge(s["zero"], 1)
            pool.affine_select(out=ident[:, :], in_=ident[:, :], compare_op=ALU.not_equal, fill=1.0, base=0,
                               pattern=[[-1, 128]], channel_multiplier=1).then_inc(s["ident_ready"], 1)
            pool.memset(mhalf[:, :], -0.5).then_inc(s["consts"], 1)
            pool.memset(cap[:, :], CAP).then_inc(s["consts"], 1)
            for e in range(NE):
                pool.memset(rev[:, e:e + 1], float(NE - e)).then_inc(s["consts"], 1)
            pool.memset(run_m[:, 0:1], 0.0).then_inc(s["consts"], 1)
            pool.memset(g_w[:, :], 0.0).then_inc(s["consts"], 1)
            pool.wait_ge(s["consts"], 12)

            def rsqrt(dst, src, given, done, q):
                pool.wait_ge(s[given], q + 1)
                pool.tensor_tensor(dst[:, :], src[:, :], mhalf[:, :], ALU.pow).then_inc(s[done], 1)

            def xlstm(sl, q):
                if sl == 2:
                    rsqrt(rs1, ve1, "ve1_ready", "rs1_ready", q)
                if sl == 6:
                    pool.wait_ge(s["fi_ready"], q + 1)
                    pool.tensor_tensor(g_i[:, :], g_i[:, :], cap[:, :].to_broadcast([128, T]), ALU.mult).then_inc(s["i_ready"], 1)
                if sl == 9:
                    pool.wait_ge(s["m_ready"], q + 1)
                    pool.tensor_tensor(d_f[:, :], g_r[:, :], run_m[:, 0:T], ALU.add).then_inc(s["df_sum"], 1)
                    pool.tensor_tensor(d_i[:, :], g_i[:, :], run_m[:, 1:T + 1], ALU.subtract).then_inc(s["di_ready"], 1)
                    pool.wait_ge(s["df_sum"], q + 1)
                    pool.tensor_tensor(d_f[:, :], d_f[:, :], run_m[:, 1:T + 1], ALU.subtract).then_inc(s["df_ready"], 1)
                if sl == 12:
                    pool.wait_ge(s["oz_ready"], q + 1)
                    pool.tensor_tensor(i_z[:, :], s_i[:, :], g_z[:, :], ALU.mult).then_inc(s["iz_ready"], 1)

            def routing(sl, q):
                if sl == 2:
                    rsqrt(rms, ms, "ms_ready", "rms_ready", q)
                if sl == 4:
                    rsqrt(rs2, ve2, "ve2_ready", "rs2_ready", q)
                if sl == 7:
                    rsqrt(rs3, ve3, "ve3_ready", "rs3_ready", q)
                if sl == 8:
                    pool.wait_ge(s["hrn_ready"], 2 * q + 2)
                    pool.tensor_tensor(tile2(hr_g[:, :]), tile2(hr_n[:, :]), over_tiles(lng_bc[:, :]), ALU.mult).then_inc(s["hrg_ready"], 1)
                    pool.wait_ge(s["hrg_ready"], q + 1)
                    pool.tensor_tensor(tile2(hr_b[:, :]), tile2(hr_g[:, :]), over_tiles(lnb_bc[:, :]), ALU.add).then_inc(s["hrb_ready"], 1)

            def scaled(b, u):
                n = UNITS * b + u
                pool.wait_ge(s["fac_ready"], n + 1)
                for h in range(2):
                    p = tile2(prob[u % 4][:, h * 512:(h + 1) * 512])
                    pool.tensor_tensor(p, p, bc(fac[:, (u % 4) * 4 + 2 * h:(u % 4) * 4 + 2 * h + 2], T),
                                       ALU.mult).then_inc(s["scaled_ready"], 1)

            def summed(b, p):
                n = PAIRS * b + p
                pool.wait_ge(s["om_ready"], n + 2)
                if p == 0:
                    pool.wait_ge(s["out_ps"], b + 1)
                pool.tensor_tensor(o_sum[:, p * T:(p + 1) * T], o_m[:, 0:T], o_m[:, T:2 * T],
                                   ALU.add).then_inc(s["osum_ready"], 1)

            def attention(b, q2, q1):
                last = q2 is None
                for sl in range(2, UNITS + 2):
                    if q2 is not None and sl == 8:
                        routing(sl, q2)
                    if sl - 1 < UNITS:
                        scaled(b, sl - 1)
                    elif not last:
                        scaled(b + 1, sl - 1 - UNITS)
                    if sl > 2 and sl % 2 == 0:
                        summed(b, (sl - 4) // 2)
                    if q2 is not None and sl != 8:
                        routing(sl, q2)
                    if q1 is not None:
                        xlstm(sl, q1)
                summed(b, PAIRS - 1)

            for sl in range(2, UNITS + 2):
                xlstm(sl, 0)
            pool.wait_ge(s["w_small"], 16 * NSMALL)
            for sl in range(2, UNITS + 2):
                routing(sl, 0)
                xlstm(sl, 1)
            scaled(0, 0)
            with pool.Fori(0, B - 2) as b:
                attention(b, b + 1, b + 2)
            attention(B - 2, B - 1, None)
            attention(B - 1, None, None)

        @block.scalar
        def _(act):
            act.sem_inc(s["pT_ready"], 2)
            act.dma_start(w_gates[:, :], W).then_inc(s["w_first"], 16)
            act.dma_start(b_gates[:, :], b4).then_inc(s["w_first"], 16)
            act.dma_start(b_in[:, :], ib).then_inc(s["w_first"], 16)
            act.wait_ge(s["w_first"], 16 * 3)
            act.activation(b_ti[:, :], b_in[:, :], ACT.Identity, bias=b_gates[:, 0:1]).then_inc(s["b_ready"], 1)
            act.wait_ge(s["b_ready"], 1)
            act.mul(b_ti[:, :], b_ti[:, :], 1.0 / CAP).then_inc(s["b_ready"], 1)
            act.mul(b_no[:, :], b_gates[:, 2:3], -1.0).then_inc(s["b_ready"], 1)
            act.wait_ge(s["b_ready"], 3)

            def xlstm_psum(sl, q):
                if sl == 4:
                    act.wait_ge(s["xn_ps"], q + 1)
                    act.activation(x_nT[:, :], ps_m[:, 0:T], ACT.Copy).then_inc(s["xnT_ready"], 1)
                if sl == 5:
                    act.wait_ge(s["fi_ps"], q + 1)
                    act.activation(g_r[:, :], ps_m[:, 0:T], ACT.Relu, bias=b_gates[:, 1:2])
                    act.activation(g_a[:, :], ps_m[:, 0:T], ACT.Abs, bias=b_gates[:, 1:2]).then_inc(s["a_ready"], 1)
                    act.activation(g_i[:, :], ps_m[:, T:2 * T], ACT.Tanh, bias=b_ti[:, 0:1],
                                   scale=1.0 / CAP).then_inc(s["fi_ready"], 1)
                if sl == 11:
                    act.wait_ge(s["oz_ps"], q + 1)
                    act.activation(g_o[:, :], ps_m[:, 0:T], ACT.Exp, bias=b_no[:, 0:1], scale=-1.0)
                    act.activation(g_z[:, :], ps_m[:, T:2 * T], ACT.Tanh, bias=b_gates[:, 3:4]).then_inc(s["oz_ready"], 1)

            def xlstm_sbuf(sl, q):
                if sl == 7:
                    act.wait_ge(s["ea_ready"], q + 1)
                    act.activation(g_a[:, :], g_a[:, :], ACT.Ln, bias=1.0).then_inc(s["ln_ready"], 1)
                if sl == 6:
                    act.wait_ge(s["a_ready"], q + 1)
                    act.activation(g_a[:, :], g_a[:, :], ACT.Exp, scale=-1.0).then_inc(s["ea_ready"], 1)
                if sl == 10:
                    act.wait_ge(s["di_ready"], q + 1)
                    act.activation(s_i[:, :], d_i[:, :], ACT.Exp).then_inc(s["si_ready"], 1)
                    act.wait_ge(s["df_ready"], q + 1)
                    act.activation(s_f[:, :], d_f[:, :], ACT.Exp).then_inc(s["sf_ready"], 1)

            def xlstm(sl, q):
                xlstm_psum(sl, q)
                xlstm_sbuf(sl, q)

            def gates_t(q, bank):
                act.wait_ge(s["gT_ps"], q + 1)
                act.activation(g_T[:, :], bank[0:NE, 0:T], ACT.Copy).then_inc(s["gT_ready"], 1)

            def routing(sl, q):
                if sl == 2:
                    act.wait_ge(s["h_ps"], q + 1)
                    for j in range(2):
                        act.activation(sq[:, j * 128:(j + 1) * 128], ps_m[:, j * 128:(j + 1) * 128], ACT.Square,
                                       accum_out=ssq[:, j:j + 1]).then_inc(s["ssq_ready"], 1)
                    act.activation(h_tok[:, :], ps_m[:, 0:T], ACT.Copy).then_inc(s["htok_ready"], 1)
                if sl == 6:
                    act.wait_ge(s["xn2_ps"], q + 1)
                    act.activation(x_hT[:, :], ps_m[:, 0:T], ACT.Copy).then_inc(s["xhT_ready"], 1)
                if sl == 9:
                    act.wait_ge(s["hrT_ps"], q + 1)
                    act.activation(hr_T[:, :], ps_m[:, 0:128], ACT.Relu).then_inc(s["hrT_ready"], 1)
                if sl == 12:
                    act.wait_ge(s["diff_ready"], q + 1)
                    act.activation(ediff[:, :], diff[:, :], ACT.Exp).then_inc(s["ediff_ready"], 1)
                if sl == 16:
                    gates_t(q, ps_m)
                if sl == 14:
                    if later(q):
                        act.wait_ge(s["v_ps"], PAIRS * q)
                    act.activation(x_cur[:, :], x_hT[:, :], ACT.Copy).then_inc(s["xcur_ready"], 1)

            def exps(b, u):
                n = UNITS * b + u
                act.wait_ge(s["negmax_ready"], n + 1)
                for c in range(4):
                    act.activation(prob[u % 4][:, c * T:(c + 1) * T], ps_s[u % 2][:, c * T:(c + 1) * T], ACT.Exp,
                                   bias=negmax[:, (u % 4) * 4 + c:(u % 4) * 4 + c + 1],
                                   accum_out=den[:, (u % 4) * 4 + c:(u % 4) * 4 + c + 1]).then_inc(s["probs_ready"], 1)

            def to_sbuf(b, u, h):
                n = UNITS * b + u
                act.wait_ge(s["pT_ps"], 2 * n + 1 + h)
                act.activation(probT[u % 2][:, h * 512:(h + 1) * 512], ps_t[h][:, :], ACT.Copy).then_inc(s["pT_ready"], 1)

            def attention(b, q2, q1):
                for sl in range(2, UNITS + 2):
                    if q2 is not None and sl == 14:
                        routing(sl, q2)
                    to_sbuf(b, sl - 2, 0)
                    if q2 is not None and sl != 14:
                        routing(sl, q2)
                    if q1 is not None:
                        xlstm_psum(sl, q1)
                    to_sbuf(b, sl - 2, 1)
                    if q1 is not None:
                        xlstm_sbuf(sl, q1)
                    if sl < UNITS:
                        exps(b, sl)
                    elif q2 is not None:
                        exps(b + 1, sl - UNITS)

            for sl in range(2, UNITS + 2):
                xlstm(sl, 0)
            act.wait_ge(s["w_small"], 16 * NSMALL)
            act.mul(k_b[:, :], k_b[:, :], SCALE).then_inc(s["kb_ready"], 1)
            for sl in range(2, 15):
                routing(sl, 0)
                xlstm(sl, 1)
            gates_t(0, ps_v)
            exps(0, 0)
            exps(0, 1)
            with act.Fori(0, B - 2) as b:
                attention(b, b + 1, b + 2)
            attention(B - 2, B - 1, None)
            attention(B - 1, None, None)

        @block.vector
        def _(dve):
            dve.sem_inc(s["y_ready"], 1)
            dve.sem_inc(s["om_ready"], 1)
            dve.memset(rw2[:, :], 0.0).then_inc(s["tail_zero"], 1)

            def moments(st, mv, ve, src, width, n_stats, n_mv, n_ve, q):
                for j in range(2):
                    dve.bn_stats(st[:, 6 * j:6 * j + 6], src[j]).then_inc(s[n_stats], 1)
                dve.wait_ge(s[n_stats], 2 * q + 2)
                dve.memset(fence[:, :], 0.0)
                for j in range(2):
                    dve.bn_aggr(mv[:, 2 * j:2 * j + 2], st[:, 6 * j:6 * j + 6]).then_inc(s[n_mv], 1)
                dve.wait_ge(s[n_mv], 2 * q + 2)
                dve.tensor_scalar(ve[:, :], tile2(mv[:, :])[:, :, 1], 1e-5, None, ALU.add).then_inc(s[n_ve], 1)

            def x_tiles(q):
                return [xs[:, bass.ds(q * 2 * D + j * D, D)] for j in range(2)]

            def xlstm(sl, q):
                if sl == 2:
                    moments(st1, mv1, ve1, x_tiles(q), D, "stats1", "mv1_ready", "ve1_ready", q)
                if sl == 3:
                    dve.wait_ge(s["rs1_ready"], q + 1)
                    for j in range(2):
                        dve.tensor_scalar(x_n[:, j * D:(j + 1) * D], x_tiles(q)[j], mv1[:, 2 * j:2 * j + 1],
                                          rs1[:, j:j + 1], ALU.subtract, ALU.mult).then_inc(s["xn_ready"], 1)
                if sl == 8:
                    dve.wait_ge(s["ln_ready"], q + 1)
                    dve.scalar_tensor_tensor(g_r[:, :], g_r[:, :], -1.0, g_a[:, :], ALU.mult,
                                             ALU.subtract).then_inc(s["f_ready"], 1)
                    dve.wait_ge(s["i_ready"], q + 1)
                    dve.wait_ge(s["f_ready"], q + 1)
                    dve.tensor_tensor_scan(run_m[:, 1:T + 1], g_r[:, :], g_i[:, :], 0.0, ALU.add,
                                           ALU.max).then_inc(s["m_ready"], 1)
                if sl == 12:
                    dve.wait_ge(s["sf_ready"], q + 1)
                    dve.tensor_tensor_scan(run_n[:, :], s_f[:, :], s_i[:, :], 0.0, ALU.mult, ALU.add).then_inc(s["n_ready"], 1)
                    dve.wait_ge(s["n_ready"], q + 1)
                    dve.tensor_scalar(run_n[:, :], run_n[:, :], 1e-6, None, ALU.add).then_inc(s["ne_ready"], 1)
                if sl == 13:
                    dve.wait_ge(s["ne_ready"], q + 1)
                    dve.wait_ge(s["oz_ready"], q + 1)
                    dve.scalar_tensor_tensor(dn[:, :], g_o[:, :], 1.0, run_n[:, :], ALU.add, ALU.mult).then_inc(s["dn_ready"], 1)
                if 14 <= sl < 18:
                    k = sl - 14
                    if k == 0:
                        dve.wait_ge(s["dn_ready"], q + 1)
                    dve.reciprocal(rdn[:, k * 64:(k + 1) * 64], dn[:, k * 64:(k + 1) * 64]).then_inc(s["rdn_ready"], 1)
                if sl == 16:
                    dve.wait_ge(s["iz_ready"], q + 1)
                    dve.tensor_tensor_scan(run_c[:, :], s_f[:, :], i_z[:, :], 0.0, ALU.mult, ALU.add).then_inc(s["c_ready"], 1)
                if sl == 17:
                    dve.wait_ge(s["c_ready"], q + 1)
                    dve.wait_ge(s["rdn_ready"], 4 * q + 4)
                    dve.tensor_tensor(hid[:, :], run_c[:, :], rdn[:, :], ALU.mult).then_inc(s["h_ready"], 1)

            steps = [0]

            def choose(rank, q):
                def step(ins):
                    steps[0] += 1
                    ins.then_inc(s["top"], 1)
                    dve.wait_ge(s["top"], TOP_STEPS * q + steps[0])
                lg3, eq3 = tile2(lg[:, :]), tile2(eq[:, :])
                o = tile2(oh[:, rank * 2 * NE:(rank + 1) * 2 * NE])
                steps[0] = 6 * rank
                top = best[:, 2 * rank:2 * rank + 2]
                step(dve.tensor_reduce(top, lg3, AX.X, ALU.max))
                step(dve.tensor_tensor(eq3, lg3, bc(top, NE), ALU.is_equal))
                step(dve.tensor_tensor(eq3, eq3, over_tiles(rev[:, :]), ALU.mult))
                step(dve.tensor_reduce(hit[:, :], eq3, AX.X, ALU.max))
                step(dve.tensor_tensor(o, eq3, bc(hit[:, :], NE), ALU.is_equal))
                if rank == 0:
                    step(dve.scalar_tensor_tensor(lg3, o, BELOW, lg3, ALU.mult, ALU.add))

            def gates(part, q):
                def step(ins):
                    steps[0] += 1
                    ins.then_inc(s["top"], 1)
                    dve.wait_ge(s["top"], TOP_STEPS * q + steps[0])
                steps[0] = 11 if part == 0 else 14
                g = [gate[:, bass.ds(r * TILES + 2 * q, 2)] for r in range(2)]
                if part == 0:
                    dve.wait_ge(s["ediff_ready"], q + 1)
                    step(dve.tensor_scalar(gsum[:, :], ediff[:, :], 1.0, None, ALU.add))
                    step(dve.reciprocal(gsum[:, :], gsum[:, :]))
                    dve.tensor_scalar(g[0], gsum[:, :], 1.0, None, ALU.mult)
                    step(dve.tensor_tensor(g[1], ediff[:, :], gsum[:, :], ALU.mult))
                else:
                    for r in range(2):
                        step(dve.tensor_tensor(tile2(g_e[:, r * 2 * NE:(r + 1) * 2 * NE]),
                                               tile2(oh[:, r * 2 * NE:(r + 1) * 2 * NE]), bc(g[r], NE), ALU.mult))
                    assert steps[0] == TOP_STEPS
                    dve.tensor_tensor(tile2(g_w[:, :])[:, :, 0:NE], tile2(g_e[:, 0:2 * NE]), tile2(g_e[:, 2 * NE:4 * NE]),
                                      ALU.add).then_inc(s["gw_ready"], 1)

            def output_bias(q, bank):
                dve.wait_ge(s["ob_ps"], q + 1)
                dve.tensor_tensor(seq(xs, q, 2 * D), seq(xs, q, 2 * D), bank[:, 0:2 * D], ALU.add).then_inc(s["ob_ready"], 1)

            def routing_first(sl, q):
                if sl == 8:
                    dve.wait_ge(s["rs3_ready"], q + 1)
                    for j in range(2):
                        dve.tensor_scalar(hr_n[:, j * R:(j + 1) * R], hr[:, j * R:(j + 1) * R], mv3[:, 2 * j:2 * j + 1],
                                          rs3[:, j:j + 1], ALU.subtract, ALU.mult).then_inc(s["hrn_ready"], 1)

            def routing_psum(sl, q):
                if sl == 2:
                    dve.wait_ge(s["ssq_ready"], 2 * q + 2)
                    dve.tensor_scalar(ms[:, :], ssq[:, :], 1.0 / D, 1e-8, ALU.mult, ALU.add).then_inc(s["ms_ready"], 1)
                if sl == 7:
                    dve.wait_ge(s["hr_ps"], q + 1)
                    dve.tensor_tensor(tile2(hr[:, :]), tile2(ps_m[:, 0:2 * R]), over_tiles(rb1_bc[:, :]),
                                      ALU.add).then_inc(s["hr_ready"], 1)
                    dve.wait_ge(s["hr_ready"], q + 1)
                    moments(st3, mv3, ve3, [hr[:, j * R:(j + 1) * R] for j in range(2)], R, "stats3", "mv3_ready", "ve3_ready", q)
                if sl == 10:
                    dve.wait_ge(s["lg_ps"], q + 1)
                    dve.tensor_tensor(tile2(lg[:, :]), tile2(ps_m[:, 0:2 * NE]), over_tiles(rb2_bc[:, :]),
                                      ALU.add).then_inc(s["lg_ready"], 1)
                if sl == 12:
                    for c in range(4):
                        src = oh[:, c * NE:(c + 1) * NE].rearrange("p (o e f) -> p o e f", o=1, f=1)
                        dst = oh_w[:, c * 128:(c + 1) * 128].rearrange("p (h e d) -> p h e d", h=2, e=NE)
                        dve.tensor_copy(dst, src.to_broadcast([128, 2, NE, DH])).then_inc(s["ohw_ready"], 1)
                if sl == 13:
                    dve.wait_ge(s["mask_ps"], q + 1)
                    dve.tensor_scalar(seq(mask, q, 2 * T), ps_m[:, :], 1.0, None, ALU.mult).then_inc(s["mask_ready"], 1)
                if sl == 17:
                    output_bias(q, ps_m)

            def routing_sbuf(sl, q):
                if sl == 3:
                    dve.wait_ge(s["htok_ready"], q + 1)
                    dve.wait_ge(s["rms_ready"], q + 1)
                    for j in range(2):
                        h_j = h_tok[:, j * D:(j + 1) * D]
                        dve.scalar_tensor_tensor(h_j, h_j, rms[:, j:j + 1], scale_bc[:, :], ALU.mult,
                                                 ALU.mult).then_inc(s["h3_ready"], 1)
                if sl == 4:
                    dve.wait_ge(s["h3_ready"], 2 * q + 2)
                    dve.tensor_tensor(seq(xs, q, 2 * D), seq(xs, q, 2 * D), h_tok[:, :], ALU.add).then_inc(s["x1_ready"], 1)
                    dve.wait_ge(s["x1_ready"], q + 1)
                    moments(st2, mv2, ve2, x_tiles(q), D, "stats2", "mv2_ready", "ve2_ready", q)
                if sl == 5:
                    dve.wait_ge(s["rs2_ready"], q + 1)
                    for j in range(2):
                        dve.tensor_scalar(x_n2[:, j * D:(j + 1) * D], x_tiles(q)[j], mv2[:, 2 * j:2 * j + 1],
                                          rs2[:, j:j + 1], ALU.subtract, ALU.mult).then_inc(s["xn2_ready"], 1)
                if sl == 10:
                    dve.wait_ge(s["lg_ready"], q + 1)
                    choose(0, q)
                if sl == 11:
                    choose(1, q)
                    dve.tensor_tensor(diff[:, :], best[:, 2:4], best[:, 0:2], ALU.subtract).then_inc(s["diff_ready"], 1)
                if sl == 14:
                    gates(0, q)
                if sl == 15:
                    gates(1, q)

            def routing(sl, q):
                routing_first(sl, q)
                routing_psum(sl, q)
                routing_sbuf(sl, q)

            def qk_evac(b, p):
                n = PAIRS * b + p
                if p == 0:
                    dve.wait_ge(s["mask_ready"], b + 1)
                dve.wait_ge(s["qk_ps"], n + 1)
                qp = ps_m[:, 0:T].rearrange("p (o t) -> p o t", o=1).to_broadcast([128, 2, T])
                dve.scalar_tensor_tensor(tile2(q_m[p % 2][:, :]), qp, q_b[:, p:p + 1], tile2(seq(mask, b, 2 * T)),
                                         ALU.add, ALU.mult)
                dve.tensor_scalar(k_m[p % 2][:, :], ps_m[:, T:2 * T], SCALE, k_b[:, p:p + 1],
                                  ALU.mult, ALU.add).then_inc(s["k_ready"], 1)

            def v_evac(b, p):
                n = PAIRS * b + p
                dve.wait_ge(s["v_ps"], n + 1)
                dve.tensor_tensor(tile2(v_m[p % 4][:, :]), tile2(ps_m[:, 0:2 * 128]),
                                  over_tiles(v_b[:, p * 128:(p + 1) * 128]), ALU.add).then_inc(s["v_ready"], 1)

            def maxes(b, u):
                n = UNITS * b + u
                dve.wait_ge(s["scores_ready"], n + 1)
                dve.tensor_reduce(negmax[:, (u % 4) * 4:(u % 4) * 4 + 4],
                                  ps_s[u % 2][:, :].rearrange("p (c k) -> p c k", c=4), AX.X, ALU.max,
                                  negate=True).then_inc(s["negmax_ready"], 1)

            def factors(b, u):
                n = UNITS * b + u
                f = fac[:, (u % 4) * 4:(u % 4) * 4 + 4]
                dve.wait_ge(s["probs_ready"], 4 * n + 4)
                dve.reciprocal(f, den[:, (u % 4) * 4:(u % 4) * 4 + 4]).then_inc(s["rden_ready"], 1)
                dve.wait_ge(s["rden_ready"], n + 1)
                g2 = gate[:, bass.ds(u % 2 * TILES + 2 * b, 2)].rearrange("p (o t) -> p o t", o=1).to_broadcast([128, 2, 2])
                dve.tensor_tensor(tile2(f), tile2(f), g2, ALU.mult).then_inc(s["fac_ready"], 1)

            def masked(b, p):
                n = PAIRS * b + p
                dve.wait_ge(s["pv_ps"], 2 * n + 2)
                dve.wait_ge(s["osum_ready"], n + 1)
                dve.tensor_tensor(o_m[:, :], ps_v[:, :], seq(mask, b, 2 * T), ALU.mult).then_inc(s["om_ready"], 1)

            def attention(b, q2, q1):
                last = q2 is None
                for sl in range(2, UNITS + 2):
                    if q2 is not None:
                        routing_first(sl, q2)
                    if sl - 1 < UNITS:
                        factors(b, sl - 1)
                    elif not last:
                        factors(b + 1, sl - 1 - UNITS)
                    if q2 is not None:
                        routing_psum(sl, q2)
                    p = sl // 2 + 1
                    evac = qk_evac if sl % 2 == 0 else v_evac
                    if sl == UNITS + 1 and not last:
                        evac(b + 1, p - PAIRS)
                    if sl < UNITS:
                        maxes(b, sl)
                    elif not last:
                        maxes(b + 1, sl - UNITS)
                    if p < PAIRS:
                        evac(b, p)
                    elif not last and sl != UNITS + 1:
                        evac(b + 1, p - PAIRS)
                    if q1 is not None and sl == 3:
                        xlstm(sl, q1)
                    if q2 is not None:
                        routing_sbuf(sl, q2)
                    if sl % 2 == 1:
                        masked(b, (sl - 2) // 2)
                    if q1 is not None and sl != 3:
                        xlstm(sl, q1)
                dve.wait_ge(s["out_ps"], b + 2)
                dve.tensor_tensor(seq(xs, b, 2 * D), ps_m[:, 0:2 * D], seq(xs, b, 2 * D), ALU.add).then_inc(s["y_ready"], 1)

            dve.wait_ge(s["x_first"], 16)
            dve.wait_ge(s["consts"], 12)
            for sl in range(2, UNITS + 2):
                xlstm(sl, 0)
            dve.wait_ge(s["w_small"], 16 * NSMALL)
            for sl in range(2, 14):
                routing(sl, 0)
                xlstm(sl, 1)
            dve.wait_ge(s["w_in"], 16 * 5)
            dve.wait_ge(s["kb_ready"], 1)
            qk_evac(0, 0)
            routing(14, 0)
            routing(15, 0)
            xlstm(14, 1)
            xlstm(15, 1)
            maxes(0, 0)
            v_evac(0, 0)
            output_bias(0, ps_v)
            factors(0, 0)
            qk_evac(0, 1)
            v_evac(0, 1)
            xlstm(16, 1)
            xlstm(17, 1)
            maxes(0, 1)
            dve.wait_ge(s["x_in"], 16 * 2)
            with dve.Fori(0, B - 2) as b:
                attention(b, b + 1, b + 2)
            attention(B - 2, B - 1, None)
            attention(B - 1, None, None)

        @block.tensor
        def _(pe):
            pe.sem_inc(s["out_ps"], 1)
            pe.wait_ge(s["ident_ready"], 1)
            pe.wait_ge(s["w_first"], 16 * 3)

            def xlstm(sl, q, alone):
                if sl == 4:
                    pe.wait_ge(s["xn_ready"], 2 * q + 2)
                    if alone and q == 1:
                        pe.wait_ge(s["htok_ready"], 1)
                    for j in range(2):
                        last = pe.transpose(ps_m[:, j * 128:(j + 1) * 128], x_n[:, j * 128:(j + 1) * 128], ident[:, :])
                    last.then_inc(s["xn_ps"], 1)
                if sl == 5:
                    pe.wait_ge(s["xnT_ready"], q + 1)
                    pe.matmul(ps_m[:, 0:T], w_gates[:, D:2 * D], x_nT[:, :], start=True, stop=True)
                    pe.matmul(ps_m[:, T:2 * T], w_gates[:, 0:D], x_nT[:, :], start=True, stop=True).then_inc(s["fi_ps"], 1)
                if sl == 11:
                    pe.wait_ge(s["fi_ready"], q + 1)
                    if alone and q == 1:
                        pe.wait_ge(s["lg_ready"], 1)
                    pe.matmul(ps_m[:, 0:T], w_gates[:, 2 * D:3 * D], x_nT[:, :], start=True, stop=True)
                    pe.matmul(ps_m[:, T:2 * T], w_gates[:, 3 * D:4 * D], x_nT[:, :], start=True, stop=True).then_inc(s["oz_ps"], 1)

            def gates_t(q, bank):
                pe.wait_ge(s["gw_ready"], q + 1)
                for j in range(2):
                    last = pe.transpose(bank[:, j * 128:(j + 1) * 128], g_w[:, j * 128:(j + 1) * 128], ident[:, :])
                last.then_inc(s["gT_ps"], 1)

            def output_bias(q, bank):
                pe.wait_ge(s["gT_ready"], q + 1)
                for j in range(2):
                    last = pe.matmul(bank[:, j * D:(j + 1) * D], g_T[:, j * 128:(j + 1) * 128], ob_w[:, :], start=True, stop=True)
                last.then_inc(s["ob_ps"], 1)

            def routing(sl, q, alone):
                if sl == 2:
                    pe.wait_ge(s["h_ready"], q + 1)
                    for j in range(2):
                        last = pe.transpose(ps_m[:, j * 128:(j + 1) * 128], hid[:, j * 128:(j + 1) * 128], ident[:, :])
                    last.then_inc(s["h_ps"], 1)
                if sl == 6:
                    pe.wait_ge(s["xn2_ready"], 2 * q + 2)
                    if alone:
                        pe.wait_ge(s["fi_ready"], 2)
                    for j in range(2):
                        last = pe.transpose(ps_m[:, j * 128:(j + 1) * 128], x_n2[:, j * 128:(j + 1) * 128], ident[:, :])
                    last.then_inc(s["xn2_ps"], 1)
                if sl == 7:
                    pe.wait_ge(s["xhT_ready"], q + 1)
                    for j in range(2):
                        last = pe.matmul(ps_m[:, j * R:(j + 1) * R], x_hT[:, j * 128:(j + 1) * 128], rw1[:, :], start=True, stop=True)
                    last.then_inc(s["hr_ps"], 1)
                if sl == 9:
                    pe.wait_ge(s["hrb_ready"], q + 1)
                    pe.transpose(ps_m[:, 0:128], hr_b[:, :], ident[:, :]).then_inc(s["hrT_ps"], 1)
                if sl == 10:
                    pe.wait_ge(s["hrT_ready"], q + 1)
                    pe.matmul(ps_m[:, 0:2 * NE], hr_T[:, :], rw2[:, :], start=True, stop=True).then_inc(s["lg_ps"], 1)
                if sl == 13:
                    pe.wait_ge(s["ohw_ready"], 4 * q + 4)
                    if alone:
                        pe.wait_ge(s["oz_ready"], 2)
                    for c in range(4):
                        last = pe.transpose(ps_m[:, c * 128:(c + 1) * 128], oh_w[:, c * 128:(c + 1) * 128], ident[:, :])
                    last.then_inc(s["mask_ps"], 1)
                if sl == 16:
                    gates_t(q, ps_m)
                if sl == 17:
                    output_bias(q, ps_m)

            routing_read = {2: "htok_ready", 6: "xhT_ready", 7: "hr_ready", 9: "hrT_ready", 10: "lg_ready",
                            13: "mask_ready", 16: "gT_ready", 17: "ob_ready"}
            xlstm_read = {4: "xnT_ready", 5: "fi_ready", 11: "oz_ready"}

            def qk_proj(b, p):
                pe.matmul(ps_m[:, 0:T], q_w[:, p * 128:(p + 1) * 128], x_cur[:, :], start=True, stop=True)
                pe.matmul(ps_m[:, T:2 * T], k_w[:, p * 128:(p + 1) * 128], x_cur[:, :], start=True,
                          stop=True).then_inc(s["qk_ps"], 1)

            def v_proj(b, p):
                pe.wait_ge(s["k_ready"], PAIRS * b + p + 1)
                for c in range(2):
                    last = pe.matmul(ps_m[:, c * 128:(c + 1) * 128], x_cur[:, c * 128:(c + 1) * 128],
                                     v_w[:, p * 128:(p + 1) * 128], start=True, stop=True)
                last.then_inc(s["v_ps"], 1)

            def scores(b, u):
                n = UNITS * b + u
                p, r = u // 2, u % 2
                if r == 0:
                    pe.wait_ge(s["k_ready"], PAIRS * b + p + 1)
                if not (isinstance(b, int) and n < 2):
                    pe.wait_ge(s["probs_ready"], 4 * (n - 1))
                for j in range(2):
                    for h in range(2):
                        last = pe.matmul(ps_s[u % 2][:, h * 512 + j * T:h * 512 + (j + 1) * T],
                                         q_m[p % 2][64 * h:64 * h + 64, r * T + j * 128:r * T + (j + 1) * 128],
                                         k_m[p % 2][64 * h:64 * h + 64, :], start=True, stop=True)
                last.then_inc(s["scores_ready"], 1)

            def to_keys(b, u):
                n = UNITS * b + u
                for h in range(2):
                    pe.wait_ge(s["scaled_ready"], 2 * n + 1 + h)
                    pe.wait_ge(s["pT_ready"], 2 * n + 1 + h)
                    for j in range(2):
                        for c in range(2):
                            last = pe.transpose(ps_t[h][:, c * T + j * 128:c * T + (j + 1) * 128],
                                                prob[u % 4][:, h * 512 + j * T + c * 128:h * 512 + j * T + (c + 1) * 128],
                                                ident[:, :])
                    last.then_inc(s["pT_ps"], 1)

            def values(b, u):
                n = UNITS * b + u
                p, r = u // 2, u % 2
                pe.wait_ge(s["pT_ready"], 2 * n + 4)
                if r == 0:
                    pe.wait_ge(s["om_ready"], PAIRS * b + p + 1)
                for c in range(2):
                    for h in range(2):
                        last = pe.matmul(ps_v[64 * h:64 * h + 64, r * T:(r + 1) * T],
                                         v_m[p % 4][:, c * 128 + 64 * h:c * 128 + 64 * h + 64],
                                         probT[u % 2][:, h * 512 + c * T:h * 512 + (c + 1) * T],
                                         start=(c == 0), stop=(c == 1))
                last.then_inc(s["pv_ps"], 1)

            def project(b):
                for p in range(PAIRS):
                    if p == 0 or p == PAIRS - 1:
                        pe.wait_ge(s["osum_ready"], PAIRS * b + (PAIRS + 1 if p else PAIRS))
                    for half in range(2):
                        last = pe.matmul(ps_m[:, half * 128:(half + 1) * 128],
                                         o_sum[:, p * T + half * 128:p * T + (half + 1) * 128],
                                         o_w[:, p * D:(p + 1) * D], start=(p == 0 and half == 0),
                                         stop=(p == PAIRS - 1), skip_group_check=True)
                last.then_inc(s["out_ps"], 1)

            def attention(b, q2, q1):
                last = q2 is None
                for sl in range(2, UNITS + 2):
                    p = sl // 2 + 1
                    n = PAIRS * b + p
                    routes, runs = q2 is not None and sl in routing_read, q1 is not None and sl in xlstm_read
                    to_keys(b, sl - 2)
                    if sl == 2:
                        pe.wait_ge(s["y_ready"], b + 1)
                    elif routes or runs or (sl % 2 == 0 and (p <= PAIRS or not last)):
                        pe.wait_ge(s["v_ready" if sl % 2 == 0 else "k_ready"], n if sl % 2 == 0 else n + 1)
                    if routes:
                        routing(sl, q2, False)
                    if runs:
                        xlstm(sl, q1, False)
                    if sl < UNITS:
                        scores(b, sl)
                    elif not last:
                        scores(b + 1, sl - UNITS)
                    if routes:
                        pe.wait_ge(s[routing_read[sl]], q2 + 1)
                    if runs:
                        pe.wait_ge(s[xlstm_read[sl]], q1 + 1)
                    proj = qk_proj if sl % 2 == 0 else v_proj
                    if p < PAIRS:
                        proj(b, p)
                    elif not last:
                        if sl == UNITS - 2:
                            pe.wait_ge(s["xcur_ready"], q2 + 1)
                        proj(b + 1, p - PAIRS)
                    values(b, sl - 2)
                if not last:
                    pe.wait_ge(s["v_ready"], PAIRS * (b + 1) + 2)
                project(b)

            for sl in range(2, UNITS + 2):
                xlstm(sl, 0, True)
            pe.wait_ge(s["w_small"], 16 * NSMALL)
            for sl in range(2, 14):
                if sl == 2:
                    pe.wait_ge(s["oz_ready"], 1)
                routing(sl, 0, True)
                xlstm(sl, 1, True)
            pe.wait_ge(s["w_in"], 16 * 5)
            pe.wait_ge(s["xcur_ready"], 1)
            pe.wait_ge(s["mask_ready"], 1)
            qk_proj(0, 0)
            scores(0, 0)
            gates_t(0, ps_v)
            v_proj(0, 0)
            output_bias(0, ps_v)
            pe.wait_ge(s["v_ready"], 1)
            qk_proj(0, 1)
            v_proj(0, 1)
            scores(0, 1)
            pe.wait_ge(s["ob_ready"], 1)
            pe.wait_ge(s["v_ready"], 2)
            with pe.Fori(0, B - 2) as b:
                attention(b, b + 1, b + 2)
            attention(B - 2, B - 1, None)
            attention(B - 1, None, None)


def kernel(**inputs):
    import numpy as np
    import concourse.bacc as bacc
    from concourse.bass_utils import run_bass_kernel_spmd
    a = {k.replace("L0_attn_", "a_").replace("L0_ffn_", "f_"): np.asarray(v) for k, v in inputs.items()}

    def by_head(w):
        return w.reshape(NE, H, DH, D).transpose(3, 1, 0, 2).reshape(D, H * NE * DH)

    def by_pair(v):
        return v.reshape(NE, PAIRS, 2, DH).transpose(2, 0, 3, 1).reshape(2 * NE * DH, PAIRS)

    arrays = {
        "x": a["a_x"], "W": a["a_W"], "b4": a["a_b"].reshape(4, D).T, "ib": a["a_input_bias"].reshape(D, 1),
        "scale": a["a_scale"].reshape(1, D), "rW1": a["f_rW1"].T, "rb1": a["f_rb1"].reshape(1, R),
        "ln_g": a["f_ln_g"].reshape(1, R), "ln_b": a["f_ln_b"].reshape(1, R), "rW2": a["f_rW2"].T,
        "rb2": a["f_rb2"].reshape(1, NE),
        "qW": by_head(a["f_qW"]), "qb": by_pair(a["f_qb"]), "kW": by_head(a["f_kW"]), "kb": by_pair(a["f_kb"]),
        "vW": by_head(a["f_vW"]), "vb": a["f_vb"].reshape(NE, H, DH).transpose(1, 0, 2).reshape(1, H * NE * DH),
        "oW": a["f_oW"].reshape(NE, D, PAIRS, 2, DH).transpose(3, 0, 4, 2, 1).reshape(2 * NE * DH, PAIRS * D),
        "ob": a["f_ob"],
    }
    arrays = {k: np.ascontiguousarray(v) for k, v in arrays.items()}
    nc = bacc.Bacc("TRN2", target_bir_lowering=False, num_devices=1)
    args = [nc.dram_tensor("in_" + k, v.shape, mybir.dt.from_np(v.dtype), kind="ExternalInput").ap()
            for k, v in arrays.items()]
    out = nc.dram_tensor("out_0", (B, T, D), fp32, kind="ExternalOutput").ap()
    xlstm_moe_attention(nc, *args, out)
    r = run_bass_kernel_spmd(nc, [{"in_" + k: v for k, v in arrays.items()}], core_ids=[0])
    return r.results[0]["out_0"]
```
